# Optimizing a Trainium2 kernel written in Bass

```python
import numpy as np
import jax
import jax.numpy as jnp

def _softmax(x, axis=-1):
    return jax.nn.softmax(x, axis=axis)

def _gelu(x):
    return jax.nn.gelu(x, approximate=True)

def _silu(x):
    return jax.nn.silu(x)

def _sigmoid(x):
    return jax.nn.sigmoid(x)

def _layernorm(x, axis=-1, eps=1e-05):
    m = jnp.mean(x, axis=axis, keepdims=True)
    v = jnp.var(x, axis=axis, keepdims=True)
    return (x - m) / jnp.sqrt(v + eps)

def _scatter_add(tgt, idx, src, axis=0):
    return tgt.at[idx].add(src)

def _segment_sum(src, seg, n):
    return jax.ops.segment_sum(src, seg, n)
kernel_name = 'mk_gnn_resnorm_d1_gnn_r8_dda236'

def setup_inputs(seed: int=0):
    np.random.seed(seed)
    _w = jnp.asarray

    def _rec_inputs():
        import jax
        import jax.numpy as jnp
        _gk = jax.random.key(seed)
        x = -0.0003713 + 1 * jax.random.normal(jax.random.fold_in(_gk, 1), (12500, 256), jnp.float32)
        src = jax.random.randint(jax.random.fold_in(_gk, 2), (200000,), 0, 12500, jnp.int32)
        dst = jax.random.randint(jax.random.fold_in(_gk, 3), (200000,), 0, 12500, jnp.int32)
        _o = jnp.argsort(dst, stable=True)
        src = src[_o]
        dst = dst[_o]
        return (x, src, dst)
    x, src, dst = _rec_inputs()

    def _L0_gnn_setup():
        import jax, jax.numpy as jnp
        import numpy as np
        HIDDEN = 256
        HEADS = 8
        HEAD_DIM = HIDDEN // HEADS
        N_NODES = 6250
        N_EDGES = 100000
        key = jax.random.key(seed)
        ks = jax.random.split(key, 12)
        h = jax.random.normal(ks[0], (N_NODES, HIDDEN), dtype=jnp.float32)
        row = jax.random.randint(ks[1], (N_EDGES,), 0, N_NODES, dtype=jnp.int64 if jax.config.jax_enable_x64 else jnp.int32)
        col = jax.random.randint(ks[2], (N_EDGES,), 0, N_NODES, dtype=jnp.int64 if jax.config.jax_enable_x64 else jnp.int32)

        def lin(kw, kb):
            W = jax.random.normal(kw, (HIDDEN, HIDDEN), dtype=jnp.float32) * 0.02
            b = jax.random.normal(kb, (HIDDEN,), dtype=jnp.float32) * 0.02
            return (W, b)
        Wq, bq = lin(ks[3], ks[4])
        Wk, bk = lin(ks[5], ks[6])
        Wv, bv = lin(ks[7], ks[8])
        Wo, bo = lin(ks[9], ks[10])
        return {'h': h, 'row': row, 'col': col, 'Wq': Wq, 'bq': bq, 'Wk': Wk, 'bk': bk, 'Wv': Wv, 'bv': bv, 'Wo': Wo, 'bo': bo}
    _L0_gnn_all = _L0_gnn_setup()
    _L0_gnn_in = {k: v for k, v in _L0_gnn_all.items() if k in ('Wq', 'bq', 'Wk', 'bk', 'Wv', 'bv', 'Wo', 'bo')}
    del _L0_gnn_all
    return {'x': x, 'src': src, 'dst': dst, 'L0_gnn_Wq': _L0_gnn_in['Wq'], 'L0_gnn_bq': _L0_gnn_in['bq'], 'L0_gnn_Wk': _L0_gnn_in['Wk'], 'L0_gnn_bk': _L0_gnn_in['bk'], 'L0_gnn_Wv': _L0_gnn_in['Wv'], 'L0_gnn_bv': _L0_gnn_in['bv'], 'L0_gnn_Wo': _L0_gnn_in['Wo'], 'L0_gnn_bo': _L0_gnn_in['bo']}

def reference(x, src, dst, L0_gnn_Wq, L0_gnn_bq, L0_gnn_Wk, L0_gnn_bk, L0_gnn_Wv, L0_gnn_bv, L0_gnn_Wo, L0_gnn_bo):
    import jax
    import jax.numpy as jnp

    def _L0_gnn_ref(h, row, col, Wq, bq, Wk, bk, Wv, bv, Wo, bo):
        import jax, jax.numpy as jnp
        import numpy as np
        HIDDEN = 256
        HEADS = 8
        HEAD_DIM = HIDDEN // HEADS
        N_NODES = 6250
        N_EDGES = 100000
        N = h.shape[0]
        scaling = HEAD_DIM ** (-0.5)
        q = (h @ Wq.T + bq).reshape(N, HEAD_DIM, HEADS) * scaling
        k = (h @ Wk.T + bk).reshape(N, HEAD_DIM, HEADS)
        v = (h @ Wv.T + bv).reshape(N, HEAD_DIM, HEADS)
        s = jnp.einsum('edh,edh->eh', q[row], k[col])
        m = jax.ops.segment_max(s, row, num_segments=N)
        e = jnp.exp(s - m[row])
        z = jax.ops.segment_sum(e, row, num_segments=N)
        attn = e / z[row]
        out = jax.ops.segment_sum(attn[:, None, :] * v[col], row, num_segments=N)
        return out.reshape(N, -1) @ Wo.T + bo
    x = _layernorm(x + _L0_gnn_ref(x, src, dst, L0_gnn_Wq, L0_gnn_bq, L0_gnn_Wk, L0_gnn_bk, L0_gnn_Wv, L0_gnn_bv, L0_gnn_Wo, L0_gnn_bo), axis=-1)
    return x

_drawn_inputs = setup_inputs


def setup_inputs(seed=0):
    import zlib

    import numpy as np

    out = dict(_drawn_inputs(seed))
    spreads = {}
    factors = {'L0_gnn_Wq': 8.0,
     'L0_gnn_bq': 42.4,
     'L0_gnn_Wk': 8.0,
     'L0_gnn_bk': 64.0,
     'L0_gnn_bv': 8.0,
     'L0_gnn_bo': 2.729}
    for name, (base, spread) in spreads.items():
        noise = np.random.default_rng([zlib.crc32(name.encode()), seed]).standard_normal(out[name].shape)
        drawn = base * np.exp(spread * noise) if base else spread * noise
        out[name] = jnp.asarray(drawn.astype(out[name].dtype))
    for name, factor in factors.items():
        out[name] = (out[name] * factor).astype(out[name].dtype)
    return out
```

```python
from contextlib import ExitStack

import concourse.bass as bass
from concourse import mybir

P = 128
N, D, E = 12500, 256, 200000
HEADS = 8
HD = D // HEADS
TILES = (N + P - 1) // P
NP = TILES * P
XW = 260
VW = HEADS * (HD + 1)
KVW = D + VW
EP = 125
EF = E // EP
FBITS, PBITS = 11, 7
SF = 1 << FBITS
HALF = SF // 2
SLOTS = P * SF
ROW_SHIFT = 14
COL_MASK = (1 << ROW_SHIFT) - 1
KEY_BASE = 0x20000000
SENTINEL = KEY_BASE | (COL_MASK << ROW_SHIFT)
CH = 320
CHUNKS = EF // CH
CLIP = 1022
G = 3
C = 48
TAB = TILES + 1
U = 4
LOOPS = (int((E / P + C + TILES * (G - 1)) // G) - 1 + U - 1) // U
STEPS = LOOPS * U + 1
NEG = -3.0e30
M0 = -1.0e30
SCALE = HD ** -0.5
EPS = 1e-5
RUNG = 14
assert TILES % RUNG == 0 and C % G == 0 and EF % CH == 0

F32, I32, BF16 = mybir.dt.float32, mybir.dt.int32, mybir.dt.bfloat16
ALU = mybir.AluOpType
ACT = mybir.ActivationFunctionType
AX = mybir.AxisListType


def prepare(nc, sem, x_rows, xT, src, dst, wkvT, bkv, wqT, bq, woT, bo, kv_rows, node_rows, edge_keys, q_perm, x_perm,
            ident, ones, upper, bo_sb, wo_sb, node_id, start_f, tile_deg, gmax_i):
    with ExitStack() as ps:
        def sb(name, shape, dtype=F32):
            return ps.enter_context(nc.sbuf_tensor(name, shape, dtype))

        def pp(name, shape, dtype=F32):
            return ps.enter_context(nc.psum_tensor(name, shape, dtype))

        A = [sb("sort_a", [P, SF]), sb("sort_b", [P, SF])]
        src_sb, dst_sb = sb("src_sb", [EP, EF], I32), sb("dst_sb", [EP, EF], I32)
        hi_b, lo_b = sb("hi_b", [EP, EF], BF16), sb("lo_b", [EP, EF], BF16)
        hot_hi, hot_lo = sb("hot_hi", [EP, TILES, CH], BF16), sb("hot_lo", [EP, P, CH], BF16)
        wkv_sb, bkv_sb = sb("wkv_sb", [P, 2, 2 * D]), sb("bkv_sb", [1, 2 * D])
        wq_sb, bq_sb = sb("wq_sb", [P, 2, D]), sb("bq_sb", [1, D])
        xt_sb = sb("xt_sb", [P, 2, 2, P])
        kv_st = sb("kv_st", [P, 2, KVW])
        xg, xgT, q_st = sb("xg", [P, 2, XW]), sb("xgT", [P, 2, D]), sb("q_st", [P, 2, D])
        pid, gray, sgn_i = sb("pid", [P, 1], I32), sb("gray", [P, 1], I32), sb("sgn_i", [P, 9], I32)
        sgn = sb("sgn", [P, 9])
        O = [sb("ord_a", [P, P]), sb("ord_b", [P, P])]
        nid_f, deg, excl = sb("nid_f", [P, P]), sb("deg", [P, P]), sb("excl", [P, P])
        start_i, ord_i = sb("start_i", [P, P], I32), sb("ord_i", [P, P], I32)
        row_sum, row_max, row_off, gmax_f = (sb(x, [P, 1]) for x in ("row_sum", "row_max", "row_off", "gmax_f"))

        hist_ps, misc_ps = pp("hist_ps", [P, 512]), pp("misc_ps", [P, 512])
        kv_ps = [pp("kv_ps0", [P, 512]), pp("kv_ps1", [P, 512])]
        q_ps = [hist_ps, misc_ps]
        T_ps = [pp("T_ps0", [P, HALF]), pp("T_ps1", [P, HALF])]

        src_in, dst_in, wkv_in, wq_in, consts, digits = (sem(x) for x in ("src_in", "dst_in", "wkv_in", "wq_in", "consts", "digits"))
        hot_lo_made, hot_hi_made, hot_used = sem("hot_lo_made"), sem("hot_hi_made"), sem("hot_used")
        sort_done = sem("sort_done")
        offs_made, ord_turned, nodes_ready = sem("offs_made"), sem("ord_turned"), sem("nodes_ready")
        starts_ready, starts_out, table_out = sem("starts_ready"), sem("starts_out"), sem("table_out")
        xt_in, kv_out = [sem("xt_in0"), sem("xt_in1")], [sem("kv_out0"), sem("kv_out1")]
        kv_made, kv_staged = sem("kv_made"), sem("kv_staged")
        turned, unturned = sem("turned"), sem("unturned")
        xg_in, x_out, q_out = [sem("xg_in0"), sem("xg_in1")], [sem("x_out0"), sem("x_out1")], [sem("q_out0"), sem("q_out1")]
        xgT_made, xgT_staged, q_made, q_staged = sem("xgT_made"), sem("xgT_staged"), sem("q_made"), sem("q_staged")
        keys_out, idle_out = sem("keys_out"), sem("idle_out")

        SPAN = range(FBITS + 1, FBITS + PBITS + 1)
        QPH = TILES // len(SPAN)
        HOT_AT = {1: 0, 4: 1, 6: 2, 8: 3, 9: 4}
        at = {}
        order_T = []
        halves = []

        with nc.Block() as block:

            @block.vector
            def _(dve):
                n = [0]

                def did(ins):
                    n[0] += 1
                    ins.then_inc(sort_done, 1)

                def settle():
                    dve.wait_ge(sort_done, n[0])

                def stage(bufs, c, lo, width, bit):
                    a, b = (bufs[x][:, lo:lo + width].rearrange("p (m two j) -> p m two j", two=2, j=1 << bit) for x in (c, 1 - c))
                    settle()
                    did(dve.tensor_tensor(b[:, :, 0, :], a[:, :, 0, :], a[:, :, 1, :], ALU.min))
                    did(dve.tensor_tensor(b[:, :, 1, :], a[:, :, 0, :], a[:, :, 1, :], ALU.max))
                    return 1 - c

                def flip(t, by=-1.0):
                    settle()
                    did(dve.tensor_scalar(t, t, by, None, ALU.mult))

                def flip_after(t, width, k):
                    w = (width - 1).bit_length()
                    if k < w - 1:
                        flip(t[:, 0:width].rearrange("p (m w) -> p m w", w=4 << k)[:, :, 1 << k:3 << k])
                    elif k == w - 1:
                        flip(t[:, 0:width // 2], sgn[:, 7:8])
                        flip(t[:, width // 2:width], sgn[:, 8:9])

                def hot_chunk(c):
                    if c:
                        dve.wait_ge(hot_used, c)
                    for v in range(P):
                        last = dve.tensor_scalar(hot_lo[:, v, :], lo_b[:, c * CH:(c + 1) * CH], float(v), None, ALU.is_equal)
                    last.then_inc(hot_lo_made, 1)

                keys = A[0][0:EP, 0:EF].bitcast(I32)
                did(dve.memset(A[0][:, :].bitcast(I32), SENTINEL))
                for h in range(2):
                    did(dve.memset(kv_st[:, h, D:KVW].rearrange("p (g w) -> p g w", w=HD + 1)[:, :, HD:HD + 1], 1.0))
                at["ones"] = n[0]
                dve.wait_ge(src_in, 16)
                did(dve.tensor_scalar(A[1][0:EP, 0:EF].bitcast(I32), src_sb[:, :], PBITS, None, ALU.logical_shift_right))
                settle()
                dve.tensor_copy(hi_b[:, :], A[1][0:EP, 0:EF].bitcast(I32)).then_inc(digits, 1)
                dve.wait_ge(digits, 1)
                did(dve.tensor_scalar(A[1][0:EP, 0:EF].bitcast(I32), src_sb[:, :], P - 1, None, ALU.bitwise_and))
                settle()
                dve.tensor_copy(lo_b[:, :], A[1][0:EP, 0:EF].bitcast(I32)).then_inc(digits, 1)
                did(dve.tensor_scalar(keys, src_sb[:, :], ROW_SHIFT, KEY_BASE, ALU.logical_shift_left, ALU.bitwise_or))
                dve.wait_ge(dst_in, 16)
                settle()
                did(dve.tensor_tensor(keys, keys, dst_sb[:, :], ALU.bitwise_or))
                dve.wait_ge(consts, 7)
                did(dve.tensor_scalar(gray[:, :], pid[:, :], 1, None, ALU.logical_shift_right))
                settle()
                did(dve.tensor_tensor(gray[:, :], gray[:, :], pid[:, :], ALU.bitwise_xor))
                settle()
                for a in range(PBITS):
                    did(dve.tensor_scalar(sgn_i[:, a:a + 1], gray[:, :], a, 1, ALU.logical_shift_right, ALU.bitwise_and))
                did(dve.tensor_scalar(sgn_i[:, 7:8], pid[:, :], 1, None, ALU.bitwise_and))
                settle()
                did(dve.tensor_scalar(sgn[:, 0:8], sgn_i[:, 0:8], -2.0, 1.0, ALU.mult, ALU.add))
                settle()
                did(dve.tensor_scalar(sgn[:, 8:9], sgn[:, 7:8], -1.0, None, ALU.mult))
                dve.wait_ge(digits, 2)

                flip(A[0][:, :].rearrange("p (m w) -> p m w", w=4)[:, :, 2:4])
                c = 0
                for k in range(1, FBITS + 1):
                    if k in HOT_AT:
                        hot_chunk(HOT_AT[k])
                    for bit in range(k - 1, -1, -1):
                        c = stage(A, c, 0, SF, bit)
                    if k < FBITS:
                        flip_after(A[c], SF, k)
                for h in range(2):
                    flip(A[c][:, h * HALF:(h + 1) * HALF], sgn[:, 0:1])
                at[FBITS + 1, "to", 0] = at[FBITS + 1, "to", 1] = n[0]

                dve.wait_ge(hot_used, CHUNKS)
                did(dve.memset(deg[:, :], 0.0))
                settle()
                did(dve.tensor_copy(deg[0:TILES, :], hist_ps[0:TILES, 0:P]))
                settle()
                did(dve.tensor_tensor_scan(excl[:, :], ones[:, :], deg[:, :], 0.0, ALU.mult, ALU.add))
                did(dve.tensor_reduce(row_max[:, :], deg[:, :], AX.X, ALU.max))
                settle()
                did(dve.tensor_copy(row_sum[:, :], excl[:, P - 1:P]))
                at["row_sum"] = n[0]
                settle()
                did(dve.tensor_tensor(excl[:, :], excl[:, :], deg[:, :], ALU.subtract))
                dve.wait_ge(offs_made, 1)
                did(dve.tensor_copy(row_off[:, :], misc_ps[:, 256:257]))
                did(dve.tensor_reduce(gmax_f[0:1, :], misc_ps[0:1, 128:256], AX.X, ALU.max))
                settle()
                did(dve.tensor_copy(gmax_i[:, :], gmax_f[0:1, :]))
                dve.tensor_scalar(start_i[:, :], excl[:, :], row_off[:, :], None, ALU.add).then_inc(starts_ready, 1)
                did(dve.tensor_scalar(deg[:, :], deg[:, :], float(CLIP), -1.0, ALU.min, ALU.mult))
                did(dve.tensor_scalar(O[1][:, :], nid_f[:, :], float(N), float((CLIP + 1) << ROW_SHIFT), ALU.is_ge, ALU.mult))
                settle()
                did(dve.tensor_scalar(deg[:, :], deg[:, :], float(CLIP), float(1 << ROW_SHIFT), ALU.add, ALU.mult))
                settle()
                did(dve.tensor_tensor(deg[:, :], deg[:, :], O[1][:, :], ALU.max))
                settle()
                did(dve.tensor_tensor(O[0][:, :], deg[:, :], nid_f[:, :], ALU.add))
                flip(O[0][:, :].rearrange("p (m w) -> p m w", w=4)[:, :, 2:4])
                o = 0

                def turn(o):
                    order_T.append((o, n[0]))
                    dve.wait_ge(ord_turned, len(order_T))
                    did(dve.tensor_copy(O[1 - o][:, :], misc_ps[:, 0:P]))
                    return 1 - o

                for k in range(1, 2 * PBITS + 1):
                    if k > PBITS:
                        o = turn(o)
                        for bit in range(k - PBITS - 1, -1, -1):
                            o = stage(O, o, 0, P, bit)
                        o = turn(o)
                    for bit in range(min(k, PBITS) - 1, -1, -1):
                        o = stage(O, o, 0, P, bit)
                    if k < PBITS:
                        flip_after(O[o], P, k)
                    elif k < 2 * PBITS:
                        flip(O[o][:, :], sgn[:, k - PBITS:k - PBITS + 1])
                settle()
                did(dve.tensor_copy(sgn_i[:, 8:9], O[o][:, 0:1]))
                o = turn(o)
                settle()
                did(dve.tensor_copy(ord_i[:, :], O[o][:, :]))
                settle()
                dve.tensor_scalar(node_id[:, :], ord_i[:, :], COL_MASK, None, ALU.bitwise_and).then_inc(nodes_ready, 1)
                did(dve.tensor_scalar(sgn_i[:, 8:9], sgn_i[:, 8:9], ROW_SHIFT, None, ALU.logical_shift_right))
                settle()
                did(dve.tensor_copy(tile_deg[:, :], sgn_i[:, 8:9]))
                settle()
                did(dve.tensor_scalar(tile_deg[:, :], tile_deg[:, :], -1.0, float(CLIP), ALU.mult, ALU.add))
                settle()
                did(dve.tensor_scalar(row_max[:, :], tile_deg[:, :], float(CLIP), float(E), ALU.is_ge, ALU.mult))
                settle()
                did(dve.tensor_tensor(tile_deg[:, :], tile_deg[:, :], row_max[:, :], ALU.add))

                for k in SPAN:
                    there = 1 - c
                    for h in range(2):
                        o = there
                        dve.wait_ge(unturned, 4 * (k - SPAN[0]) + h + 1)
                        for bit in range(k - FBITS - 1, -1, -1):
                            o = stage(A, o, h * HALF, HALF, bit)
                        at[k, "back", h] = n[0]
                    halves.append(((c, there), (o, 1 - o)))
                    c = 1 - o
                    dve.wait_ge(unturned, 4 * (k - SPAN[0]) + 4)
                    c = stage(A, c, 0, SF, FBITS - 1)
                    for h in range(2):
                        o = c
                        for bit in range(FBITS - 2, -1, -1):
                            o = stage(A, o, h * HALF, HALF, bit)
                        if k != SPAN[-1]:
                            flip(A[o][:, h * HALF:(h + 1) * HALF], sgn[:, k - FBITS:k - FBITS + 1])
                            at[k + 1, "to", h] = n[0]
                    c = o
                at["keys"] = (n[0], c)

            @block.sync
            def _(sp):
                sp.dma_start(src_sb[:, :], src).then_inc(src_in, 16)
                sp.dma_start(dst_sb[:, :], dst).then_inc(dst_in, 16)
                sp.dma_start(wkv_sb[:, :, :], wkvT).then_inc(wkv_in, 16)
                sp.dma_start(bkv_sb[:, :], bkv).then_inc(wkv_in, 16)
                for to, what in ((wq_sb[:, :, :], wqT), (bq_sb[:, :], bq), (wo_sb[:, :, :], woT), (bo_sb[:, :], bo)):
                    sp.dma_start(to, what).then_inc(wq_in, 16)
                sp.dma_start(node_rows, x_rows).then_inc(table_out, 16)
                for h in range(2):
                    sp.dma_start(xt_sb[:, h, :, :], xT[:, :, h * P:(h + 1) * P]).then_inc(xt_in[h], 16)
                with sp.Fori(0, TILES // 2 - 1) as i:
                    for h in range(2):
                        sp.wait_ge(kv_staged, 4 * i + 2 * h + 2)
                        sp.dma_start(kv_rows[bass.ds(i * (2 * P) + h * P, P), :], kv_st[:, h, :]).then_inc(kv_out[h], 16)
                        sp.dma_start(xt_sb[:, h, :, :], xT[:, :, bass.ds(i * (2 * P) + (h + 2) * P, P)]).then_inc(xt_in[h], 16)
                for h in range(2):
                    t = TILES - 2 + h
                    sp.wait_ge(kv_staged, 2 * t + 2)
                    sp.dma_start(kv_rows[t * P:(t + 1) * P, :], kv_st[:, h, :]).then_inc(kv_out[h], 16)
                sp.wait_ge(starts_ready, 1)
                sp.wait_ge(table_out, 16)
                sp.dma_start(node_rows[:, D:D + 1].rearrange("(p f) one -> p (f one)", f=P),
                             start_i[0:TILES, :].bitcast(F32), allow_slow_non_contiguous=True).then_inc(starts_out, 16)
                sp.dma_start(q_perm[NP:NP + P, :], x_rows[0:P, 0:D]).then_inc(idle_out, 16)
                with sp.Fori(0, TILES // 2) as i:
                    for h in range(2):
                        sp.wait_ge(q_staged, 4 * i + 2 * h + 2)
                        sp.dma_start(q_perm[bass.ds(i * (2 * P) + h * P, P), :], q_st[:, h, :]).then_inc(q_out[h], 16)
                        sp.dma_start(x_perm[bass.ds(i * (2 * P) + h * P, P), :], xg[:, h, 0:D]).then_inc(x_out[h], 16)
                sp.wait_ge(sort_done, at["keys"][0])
                sp.dma_start(edge_keys.rearrange("(p f) one -> p (f one)", f=SF), A[at["keys"][1]][:, :].bitcast(I32)).then_inc(keys_out, 16)
                sp.wait_ge(idle_out, 16)
                sp.wait_ge(keys_out, 16)
                for h in range(2):
                    for s in (kv_out, q_out, x_out):
                        sp.wait_ge(s[h], 16 * TILES // 2)

            @block.gpsimd
            def _(pool):
                pool.memset(ident[:, :], 0.0).then_inc(consts, 1)
                pool.memset(upper[:, :], 1.0).then_inc(consts, 1)
                pool.memset(ones[:, :], 1.0).then_inc(consts, 1)
                pool.wait_ge(consts, 3)
                pool.affine_select(out=ident[:, :], in_=ident[:, :], compare_op=ALU.not_equal, fill=1.0, base=0,
                                   pattern=[[-1, P]], channel_multiplier=1).then_inc(consts, 1)
                pool.affine_select(out=upper[:, :], in_=upper[:, :], compare_op=ALU.is_gt, fill=0.0, base=0,
                                   pattern=[[1, P]], channel_multiplier=-1).then_inc(consts, 1)
                pool.iota(pid[:, :], pattern=[[0, 1]], base=0, channel_multiplier=1).then_inc(consts, 1)
                pool.iota(nid_f[:, :], pattern=[[1, P]], base=0, channel_multiplier=P,
                          allow_small_or_imprecise_dtypes=True).then_inc(consts, 1)
                pool.wait_ge(digits, 2)
                for c in range(CHUNKS):
                    if c:
                        pool.wait_ge(hot_used, c)
                    for v in range(TILES):
                        last = pool.tensor_scalar(hot_hi[:, v, :], hi_b[:, c * CH:(c + 1) * CH], float(v), None, ALU.is_equal)
                    last.then_inc(hot_hi_made, 1)
                pool.wait_ge(nodes_ready, 1)
                pool.wait_ge(starts_out, 16)
                for i in range(TILES):
                    if i >= 2:
                        pool.wait_ge(x_out[i % 2], 16 * (i // 2))
                    pool.indirect_dma_start(out=xg[:, i % 2, :], out_offset=None, in_=node_rows,
                                            in_offset=bass.IndirectOffsetOnAxis(ap=node_id[:, i:i + 1], axis=0),
                                            bounds_check=NP - 1, oob_is_err=False).then_inc(xg_in[i % 2], 16)

            @block.tensor
            def _(pe):
                def count_chunk(c):
                    pe.wait_ge(hot_lo_made, c + 1)
                    pe.wait_ge(hot_hi_made, c + 1)
                    for e in range(CH):
                        last = pe.matmul(hist_ps[0:TILES, 0:P], hot_hi[:, :, e], hot_lo[:, :, e],
                                         start=c == 0 and e == 0, stop=c == CHUNKS - 1 and e == CH - 1)
                    last.then_inc(hot_used, 1)

                def project_kv(i, h, first=False):
                    pe.wait_ge(xt_in[h], 16 * i + 16)
                    if not first:
                        pe.wait_ge(kv_staged, 4 * i + 2 * h - 2)
                    for kc in range(2):
                        pe.matmul(kv_ps[h][:, :], xt_sb[:, h, kc, :], wkv_sb[:, kc, :], start=kc == 0, stop=False)
                    pe.matmul(kv_ps[h][:, :], ones[0:1, :], bkv_sb[0:1, :], start=False, stop=True).then_inc(kv_made, 1)

                pe.wait_ge(consts, 7)
                pe.wait_ge(wkv_in, 32)
                cuts = [1] + [round(TILES // 2 * (c + 1) / CHUNKS) for c in range(CHUNKS)]
                for c in range(CHUNKS):
                    count_chunk(c)
                    if c == 0:
                        for h in range(2):
                            project_kv(0, h, first=True)
                    with pe.Fori(cuts[c], cuts[c + 1]) as i:
                        for h in range(2):
                            project_kv(i, h)
                pe.wait_ge(sort_done, at["row_sum"])
                pe.matmul(misc_ps[:, 256:257], upper[:, :], row_sum[:, :], start=True, stop=True)
                pe.matmul(misc_ps[0:1, 128:256], row_max[:, :], ident[:, :], start=True, stop=True).then_inc(offs_made, 1)
                for o, value in order_T:
                    pe.wait_ge(sort_done, value)
                    pe.transpose(misc_ps[:, 0:P], O[o][:, :], ident[:, :]).then_inc(ord_turned, 1)

                def turn_half(k, way, h):
                    pe.wait_ge(sort_done, at[k, way, h])
                    a = A[halves[k - SPAN[0]][way == "back"][0]]
                    for b in range(HALF // P):
                        last = pe.transpose(T_ps[h][:, b * P:(b + 1) * P], a[:, h * HALF + b * P:h * HALF + (b + 1) * P], ident[:, :])
                    last.then_inc(turned, 1)

                def project_q(i, first=False):
                    for h in range(2):
                        pe.wait_ge(xg_in[h], 16 * i + 16)
                        for kc in range(2):
                            last = pe.transpose(kv_ps[h][:, kc * P:(kc + 1) * P], xg[:, h, kc * P:(kc + 1) * P], ident[:, :])
                        last.then_inc(xgT_made, 1)
                    for h in range(2):
                        pe.wait_ge(xgT_staged, 2 * i + h + 1)
                        if not first:
                            pe.wait_ge(q_staged, 4 * i + 2 * h - 2)
                        for kc in range(2):
                            pe.matmul(q_ps[h][:, 0:D], xgT[:, h, kc * P:(kc + 1) * P], wq_sb[:, kc, :], start=kc == 0, stop=False)
                        pe.matmul(q_ps[h][:, 0:D], ones[0:1, :], bq_sb[0:1, :], start=False, stop=True).then_inc(q_made, 1)

                pe.wait_ge(wq_in, 64)
                for k in SPAN:
                    for way in ("to", "back"):
                        for h in range(2):
                            turn_half(k, way, h)
                    i0 = QPH // 2 * (k - SPAN[0])
                    if i0 == 0:
                        pe.wait_ge(kv_staged, 2 * TILES)
                        project_q(0, first=True)
                    with pe.Fori(max(i0, 1), i0 + QPH // 2) as i:
                        project_q(i)

            @block.scalar
            def _(act):
                def stage_kv(i, h, first=False):
                    act.wait_ge(kv_made, 2 * i + h + 1)
                    if not first:
                        act.wait_ge(kv_out[h], 16 * i)
                    act.activation(kv_st[:, h, 0:D], kv_ps[h][:, 0:D], ACT.Copy).then_inc(kv_staged, 1)
                    act.activation(kv_st[:, h, D:KVW].rearrange("p (g w) -> p g w", w=HD + 1)[:, :, 0:HD],
                                   kv_ps[h][:, D:2 * D].rearrange("p (g w) -> p g w", w=HD), ACT.Copy).then_inc(kv_staged, 1)

                act.wait_ge(sort_done, at["ones"])
                for h in range(2):
                    stage_kv(0, h, first=True)
                with act.Fori(1, TILES // 2) as i:
                    for h in range(2):
                        stage_kv(i, h)

                def unturn_half(k, way, h, count):
                    act.wait_ge(turned, count)
                    b = A[halves[k - SPAN[0]][way == "back"][1]]
                    act.activation(b[:, h * HALF:(h + 1) * HALF], T_ps[h][:, :], ACT.Copy).then_inc(unturned, 1)

                def stage_q(i, first=False):
                    for h in range(2):
                        act.wait_ge(xgT_made, 2 * i + h + 1)
                        act.activation(xgT[:, h, :], kv_ps[h][:, 0:D], ACT.Copy).then_inc(xgT_staged, 1)
                    for h in range(2):
                        act.wait_ge(q_made, 2 * i + h + 1)
                        if not first:
                            act.wait_ge(q_out[h], 16 * i)
                        act.activation(start_f[:, bass.ds(2 * i + h, 1)], xg[:, h, D:D + 1].bitcast(I32), ACT.Copy).then_inc(q_staged, 1)
                        act.activation(q_st[:, h, :], q_ps[h][:, 0:D], ACT.Copy, scale=SCALE).then_inc(q_staged, 1)

                count = 0
                for k in SPAN:
                    for way in ("to", "back"):
                        for h in range(2):
                            count += 1
                            unturn_half(k, way, h, count)
                    i0 = QPH // 2 * (k - SPAN[0])
                    if i0 == 0:
                        stage_q(0, first=True)
                    with act.Fori(max(i0, 1), i0 + QPH // 2) as i:
                        stage_q(i)


def bounded(eng, value, most):
    return eng.snap(value).with_bounds(min_val=0, max_val=most)


def gnn_kernel(nc, x_rows, xT, src, dst, wkvT, bkv, wqT, bq, woT, bo, out):
    with ExitStack() as ctx:
        def sb(name, shape, dtype=F32):
            return ctx.enter_context(nc.sbuf_tensor(name, shape, dtype))

        def sem(name):
            return ctx.enter_context(nc.semaphore(name))

        kv_rows = nc.dram_tensor("kv_rows", (NP, KVW), F32).ap()
        node_rows = nc.dram_tensor("node_rows", (NP, XW), F32).ap()
        edge_keys = nc.dram_tensor("edge_keys", (SLOTS, 1), I32).ap()
        q_perm = nc.dram_tensor("q_perm", (TAB * P, D), F32).ap()
        x_perm = nc.dram_tensor("x_perm", (NP, D), F32).ap()

        ident, ones, upper = sb("ident", [P, P]), sb("ones", [P, P]), sb("upper", [P, P])
        wo_sb, bo_sb = sb("wo_sb", [P, 2, D]), sb("bo_sb", [1, D])
        node_id = sb("node_id", [P, P], I32)
        start_f = sb("start_f", [P, TILES])
        tile_deg = sb("tile_deg", [P, 1])
        gmax_i = sb("gmax_i", [1, 1], I32)

        prepare(nc, sem, x_rows, xT, src, dst, wkvT, bkv, wqT, bq, woT, bo, kv_rows, node_rows, edge_keys, q_perm, x_perm,
                ident, ones, upper, bo_sb, wo_sb, node_id, start_f, tile_deg, gmax_i)

        acc = sb("acc", [P, TAB * VW])
        runmax = sb("runmax", [P, TAB * HEADS])
        cols, mask = sb("cols", [P, TAB, C], I32), sb("mask", [P, TAB, C])
        step_tab = sb("step_tab", [1, STEPS + 1], I32)
        round_base = sb("round_base", [P, 1])

        acc_zeroed = sem("acc_zeroed")
        with nc.Block() as block:
            @block.vector
            def _(dve):
                dve.memset(acc[:, 0:TAB * VW // 2], 0.0)
                dve.memset(runmax[:, :], M0)
                dve.memset(round_base[:, :], 0.0)
                dve.memset(mask[:, TILES, :], NEG)
                dve.memset(cols[:, TILES, :], 0).then_inc(acc_zeroed, 1)

            @block.gpsimd
            def _(pool):
                pool.memset(acc[:, TAB * VW // 2:TAB * VW], 0.0).then_inc(acc_zeroed, 1)

        gmax = nc.values_load(gmax_i[0:1, 0:1], min_val=1, max_val=E)
        with nc.Fori(0, (gmax + (C - 1)) // C):
            one_round(nc, sem, kv_rows, edge_keys, q_perm, ident, ones, upper, node_id, start_f, tile_deg,
                      acc, runmax, cols, mask, step_tab, round_base)
        finish(nc, sem, out, x_perm, ident, ones, wo_sb, bo_sb, node_id, acc)


def one_round(nc, new_sem, kv_rows, edge_keys, q_perm, ident, ones, upper, node_id, start_f, tile_deg,
              acc, runmax, cols, mask, step_tab, round_base):
    used = []

    def sem(name):
        used.append(new_sem(name))
        return used[-1]

    with ExitStack() as ps:
        def sb(name, shape, dtype=F32):
            return ps.enter_context(nc.sbuf_tensor(name, shape, dtype))

        def pp(name, shape, dtype=F32):
            return ps.enter_context(nc.psum_tensor(name, shape, dtype))

        run_at = sb("run_at", [P, TILES], I32)
        rows = sb("rows", [P, RUNG, C], I32)
        rem, nsteps, ends = sb("rem", [P, 1]), sb("nsteps", [P, 1]), sb("ends", [P, 1])
        thresh = sb("thresh", [P, C // G])
        step_f = sb("step_f", [P, STEPS])
        past = sb("past", [P, STEPS])
        tile_tab = sb("tile_tab", [1, STEPS], I32)
        tile_f, place_f = sb("tile_f", [1, STEPS]), sb("place_f", [1, STEPS])
        idx = sb("idx", [P, U, G], I32)
        kv = sb("kv", [P, U, G, KVW])
        q = sb("q", [P, U, D])
        prod = sb("prod", [P, G, D])
        s = sb("s", [P, 2, (G + 1) * HEADS])
        pv = sb("pv", [P, 2, (G + 1) * VW])
        tab_ps = [pp("tab_ps0", [1, 512]), pp("tab_ps1", [1, 512]), pp("tab_ps2", [1, 512]), pp("tab_ps3", [1, 512])]
        end_ps = pp("end_ps", [P, 512])
        sum_ps = [pp("sum_ps0", [P, 512]), pp("sum_ps1", [P, 512])]

        plan = sem("plan")
        iotas, ends_made, counts_made, tab_ready = sem("iotas"), sem("ends_made"), sem("counts_made"), sem("tab_ready")
        runs_in = [sem(f"runs_in{i}") for i in range(TILES // RUNG)]
        run_at_ready, runs_ready = sem("run_at_ready"), sem("runs_ready")
        idx_ready, kv_in, q_in = sem("idx_ready"), [sem(f"kv_in{j}") for j in range(U)], [sem(f"q_in{j}") for j in range(U)]
        prod_made, scored, old_copied, masked, max_made, diffs_made = (
            sem(x) for x in ("prod_made", "scored", "old_copied", "masked", "max_made", "diffs_made"))
        exp_made, pv_made, carry_made, summed, acc_stored = (
            sem(x) for x in ("exp_made", "pv_made", "carry_made", "summed", "acc_stored"))
        CUT = 512
        pieces = [(a, min(a + CUT, STEPS)) for a in range(0, STEPS, CUT)]
        at = {}

        with nc.Block() as block:

            @block.vector
            def _(dve):
                n = [0]

                def did(ins):
                    n[0] += 1
                    ins.then_inc(plan, 1)

                def settle():
                    dve.wait_ge(plan, n[0])

                did(dve.tensor_scalar(rem[:, :], round_base[:, :], -1.0, None, ALU.mult))
                dve.tensor_scalar(run_at[:, :], start_f[:, :], round_base[:, :], float(SLOTS - C), ALU.add, ALU.min).then_inc(run_at_ready, 1)
                settle()
                did(dve.tensor_scalar(rem[:, :], tile_deg[:, :], rem[:, :], float(C), ALU.add, ALU.min))
                dve.wait_ge(iotas, 2)
                settle()
                did(dve.tensor_scalar(thresh[:, :], thresh[:, :], rem[:, :], None, ALU.is_lt))
                settle()
                did(dve.tensor_reduce(nsteps[:, :], thresh[:, :], AX.X, ALU.add))
                at["nsteps"] = n[0] 
                dve.wait_ge(ends_made, 1)
                did(dve.tensor_copy(ends[:, :], end_ps[:, 0:1]))
                settle()
                did(dve.tensor_scalar(past[:, :], step_f[:, :], ends[:, :], None, ALU.is_ge))
                at["past"] = n[0]
                dve.wait_ge(counts_made, 1)
                for j, (a, b) in enumerate(pieces):
                    did(dve.tensor_copy(tile_f[:, a:b], tab_ps[2 * j][:, 0:b - a]))
                    did(dve.tensor_tensor(place_f[:, a:b], step_f[0:1, a:b], tab_ps[2 * j + 1][:, 0:b - a], ALU.subtract))
                settle()
                did(dve.tensor_copy(tile_tab[:, :], tile_f[:, :]))
                did(dve.tensor_scalar(place_f[:, :], place_f[:, :], float(G), float(C - G), ALU.mult, ALU.min))
                settle()
                did(dve.scalar_tensor_tensor(place_f[:, :], tile_f[:, :], float(C), place_f[:, :], ALU.mult, ALU.add))
                settle()
                did(dve.scalar_tensor_tensor(place_f[:, :], place_f[:, :], float(P), tile_f[:, :], ALU.mult, ALU.add))
                settle()
                did(dve.memset(step_tab[:, STEPS:], TILES))
                settle()
                dve.tensor_copy(step_tab[:, 0:STEPS], place_f[:, :]).then_inc(tab_ready, 1)

                for r in range(TILES // RUNG):
                    dve.wait_ge(runs_in[r], 16 * RUNG)
                    part = cols[:, r * RUNG:(r + 1) * RUNG, :]
                    mpart = mask[:, r * RUNG:(r + 1) * RUNG, :]
                    did(dve.tensor_scalar(rows[:, :, :], part, ROW_SHIFT, COL_MASK, ALU.logical_shift_right, ALU.bitwise_and))
                    did(dve.tensor_scalar(part, part, COL_MASK, None, ALU.bitwise_and))
                    settle()
                    did(dve.tensor_tensor(mpart, rows[:, :, :],
                                          node_id[:, r * RUNG:(r + 1) * RUNG].unsqueeze(2).to_broadcast([P, RUNG, C]), ALU.not_equal))
                    settle()
                    did(dve.tensor_scalar(mpart, mpart, NEG, None, ALU.mult))
                settle()
                dve.tensor_scalar(round_base[:, :], round_base[:, :], float(C), None, ALU.add).then_inc(runs_ready, 1)

                mflat = mask[:, :, :].rearrange("p t c -> p (t c)")

                def score(k, j, b):
                    dve.wait_ge(kv_in[j], 16 * G * (k // U) + 16 * G)
                    dve.wait_ge(q_in[j], 16 * (k // U) + 16)
                    dve.tensor_tensor(prod[:, :, :], kv[:, j, :, 0:D], q[:, j, :].unsqueeze(1).to_broadcast([P, G, D]),
                                      ALU.mult).then_inc(prod_made, 1)

                def score_sum(k, b):
                    dve.wait_ge(prod_made, k + 1)
                    dve.tensor_reduce(s[:, b, 0:G * HEADS], prod[:, :, :].rearrange("p g (h d) -> p (g h) d", d=HD),
                                      AX.X, ALU.add).then_inc(scored, 1)

                def maxima(k, b, col, tile, first=False):
                    if not first:
                        dve.wait_ge(max_made, k)
                    m = runmax[:, bass.ds(tile * HEADS, HEADS)]
                    dve.tensor_copy(s[:, b, G * HEADS:], m).then_inc(old_copied, 1)
                    dve.wait_ge(scored, k + 1)
                    sv = s[:, b, 0:G * HEADS].rearrange("p (g h) -> p g h", h=HEADS)
                    dve.tensor_tensor(sv, sv, mflat[:, bass.ds(col, G)].unsqueeze(2).to_broadcast([P, G, HEADS]), ALU.add).then_inc(masked, 1)
                    dve.wait_ge(tab_ready, 1)
                    dve.wait_ge(masked, k + 1)
                    dve.wait_ge(old_copied, k + 1)
                    dve.tensor_reduce(m, s[:, b, :].rearrange("p (g h) -> p h g", h=HEADS), AX.X, ALU.max).then_inc(max_made, 1)
                    dve.wait_ge(max_made, k + 1)
                    sa = s[:, b, :].rearrange("p (g h) -> p g h", h=HEADS)
                    dve.tensor_tensor(sa, sa, m.unsqueeze(1).to_broadcast([P, G + 1, HEADS]), ALU.subtract).then_inc(diffs_made, 1)

                def weigh(k, j, b, peeled=False):
                    dve.wait_ge(exp_made, k + 1)
                    if not peeled:
                        dve.wait_ge(summed, k - 1)
                    dve.tensor_tensor(pv[:, b, 0:G * VW].rearrange("p (g h w) -> p g h w", g=G, w=HD + 1),
                                      kv[:, j, :, D:KVW].rearrange("p g (h w) -> p g h w", w=HD + 1),
                                      s[:, b, 0:G * HEADS].rearrange("p (g h) -> p g h", h=HEADS).unsqueeze(3).to_broadcast([P, G, HEADS, HD + 1]),
                                      ALU.mult).then_inc(pv_made, 1)

                def carry(k, b, tile, first=False):
                    if not first:
                        dve.wait_ge(acc_stored, k)
                    dve.tensor_tensor(pv[:, b, G * VW:].rearrange("p (h w) -> p h w", w=HD + 1),
                                      acc[:, bass.ds(tile * VW, VW)].rearrange("p (h w) -> p h w", w=HD + 1),
                                      s[:, b, G * HEADS:].unsqueeze(2).to_broadcast([P, HEADS, HD + 1]), ALU.mult).then_inc(carry_made, 1)

                dve.wait_ge(tab_ready, 1)
                dve.wait_ge(runs_ready, 1)
                tile_r = [dve.alloc_register(f"tile_{b}") for b in range(2)]
                col_r = [dve.alloc_register(f"col_{b}") for b in range(2)]

                def look_up(k, b):
                    v = dve.value_load(step_tab[0:1, bass.ds(k, 1)], min_val=0, max_val=TAB * C * P - 1)
                    dve.reg_mov(tile_r[b], v & (P - 1))
                    dve.reg_mov(col_r[b], v >> PBITS)

                def step(k, j, peel=False):
                    j1, b, b1 = (j + 1) % U, j % 2, (j + 1) % 2
                    score(k + 1, j1, b1)
                    weigh(k, j, b, peeled=peel and j < 2)
                    score_sum(k + 1, b1)
                    carry(k, b, bounded(dve, tile_r[b], TILES), first=peel and j == 0)
                    look_up(k + 2, b)
                    maxima(k + 1, b1, bounded(dve, col_r[b1], TAB * C - G), bounded(dve, tile_r[b1], TILES))

                look_up(0, 0)
                look_up(1, 1)
                score(0, 0, 0)
                score_sum(0, 0)
                maxima(0, 0, bounded(dve, col_r[0], TAB * C - G), bounded(dve, tile_r[0], TILES), first=True)
                for j in range(U):
                    step(j, j, peel=True)
                with dve.Fori(1, LOOPS) as kk:
                    for j in range(U):
                        step(kk * U + j, j)
                weigh(STEPS - 1, (STEPS - 1) % U, (STEPS - 1) % 2)
                carry(STEPS - 1, (STEPS - 1) % 2, bounded(dve, tile_r[(STEPS - 1) % 2], TILES))
                for r in tile_r + col_r:
                    dve.free_register(r)

            @block.gpsimd
            def _(pool):
                pool.iota(thresh[:, :], pattern=[[G, C // G]], base=0, channel_multiplier=0,
                          allow_small_or_imprecise_dtypes=True).then_inc(iotas, 1)
                pool.iota(step_f[:, :], pattern=[[1, STEPS]], base=0, channel_multiplier=0,
                          allow_small_or_imprecise_dtypes=True).then_inc(iotas, 1)
                pool.wait_ge(run_at_ready, 1)
                for i in range(TILES):
                    pool.indirect_dma_start(out=cols[:, i, :], out_offset=None, in_=edge_keys,
                                            in_offset=bass.IndirectOffsetOnAxis(ap=run_at[:, i:i + 1], axis=0),
                                            bounds_check=SLOTS - 1, oob_is_err=False).then_inc(runs_in[i // RUNG], 16)


                freed = pool.alloc_register("freed")
                pool.reg_mov(freed, 1)

                def gather(k, j, first=False):
                    pool.wait_ge(idx_ready, k + 1)
                    if not first:
                        pool.wait_ge(pv_made, freed)
                        pool.reg_add(freed, freed, 1)
                    for g in range(G):
                        pool.indirect_dma_start(out=kv[:, j, g, :], out_offset=None, in_=kv_rows,
                                                in_offset=bass.IndirectOffsetOnAxis(ap=idx[:, j, g:g + 1], axis=0),
                                                bounds_check=NP - 1, oob_is_err=False).then_inc(kv_in[j], 16)

                for j in range(U):
                    gather(j, j, first=True)
                with pool.Fori(1, LOOPS) as kk:
                    for j in range(U):
                        gather(kk * U + j, j)
                gather(STEPS - 1, (STEPS - 1) % U)
                pool.free_register(freed)

            @block.sync
            def _(sp):
                def load_q(k, j, first=False):
                    tile = sp.value_load(tile_tab[0:1, bass.ds(k, 1)], min_val=0, max_val=TILES)
                    if not first:
                        sp.wait_ge(prod_made, k - U + 1)
                    sp.dma_start(q[:, j, :], q_perm[bass.ds(tile * P, P), :]).then_inc(q_in[j], 16)

                sp.wait_ge(tab_ready, 1)
                for j in range(U):
                    load_q(j, j, first=True)
                with sp.Fori(1, LOOPS) as kk:
                    for j in range(U):
                        load_q(kk * U + j, j)
                load_q(STEPS - 1, (STEPS - 1) % U)

            @block.scalar
            def _(act):
                cflat = cols[:, :, :].rearrange("p t c -> p (t c)")

                def indices(k, j, first=False):
                    v = act.value_load(step_tab[0:1, bass.ds(k, 1)], min_val=0, max_val=TAB * C * P - 1)
                    col = bounded(act, v >> PBITS, TAB * C - G)
                    if not first:
                        act.wait_ge(kv_in[j], 16 * G * (k // U))
                    act.activation(idx[:, j, :], cflat[:, bass.ds(col, G)], ACT.Copy).then_inc(idx_ready, 1)

                def weights(k, b):
                    act.wait_ge(diffs_made, k + 1)
                    act.activation(s[:, b, :], s[:, b, :], ACT.Exp).then_inc(exp_made, 1)

                def store(k, b):
                    v = act.value_load(step_tab[0:1, bass.ds(k, 1)], min_val=0, max_val=TAB * C * P - 1)
                    tile = bounded(act, v & (P - 1), TILES)
                    act.wait_ge(summed, k + 1)
                    act.activation(acc[:, bass.ds(tile * VW, VW)], sum_ps[b][:, 0:VW], ACT.Copy).then_inc(acc_stored, 1)

                act.wait_ge(tab_ready, 1)
                act.wait_ge(runs_ready, 1)
                for j in range(U):
                    indices(j, j, first=True)
                weights(0, 0)
                with act.Fori(0, LOOPS - 1) as kk:
                    for j in range(U):
                        indices(kk * U + j + U, j)
                        weights(kk * U + j + 1, (j + 1) % 2)
                        store(kk * U + j, j % 2)
                indices(STEPS - 1, (STEPS - 1) % U)
                for j in range(U):
                    k = (LOOPS - 1) * U + j
                    weights(k + 1, (j + 1) % 2)
                    store(k, j % 2)
                store(STEPS - 1, (STEPS - 1) % 2)

            @block.tensor
            def _(pe):
                pe.wait_ge(plan, at["nsteps"])
                pe.matmul(end_ps[:, 0:1], upper[:, :], nsteps[:, :], start=True, stop=False)
                pe.matmul(end_ps[:, 0:1], ident[:, :], nsteps[:, :], start=False, stop=True).then_inc(ends_made, 1)
                pe.wait_ge(plan, at["past"])
                for j, (a, b) in enumerate(pieces):
                    pe.matmul(tab_ps[2 * j][:, 0:b - a], ones[0:TILES, 0:1], past[0:TILES, a:b], start=True, stop=True)
                    last = pe.matmul(tab_ps[2 * j + 1][:, 0:b - a], nsteps[0:TILES, :], past[0:TILES, a:b], start=True, stop=True)
                last.then_inc(counts_made, 1)

                def total(k, b):
                    pe.wait_ge(pv_made, k + 1)
                    for g in range(G):
                        pe.matmul(sum_ps[b][:, 0:VW], ident[:, :], pv[:, b, g * VW:(g + 1) * VW], start=g == 0, stop=False)
                    pe.wait_ge(carry_made, k + 1)
                    pe.matmul(sum_ps[b][:, 0:VW], ident[:, :], pv[:, b, G * VW:], start=False, stop=True).then_inc(summed, 1)

                with pe.Fori(0, LOOPS) as kk:
                    for j in range(U):
                        total(kk * U + j, j % 2)
                total(STEPS - 1, (STEPS - 1) % 2)

        with nc.Block() as block:

            @block.gpsimd
            def _(pool):
                numbers = range(used[0].num, used[-1].num + 1)
                assert len(numbers) == len(used)
                pool.dma_reset(numbers)
                pool.sem_clear(numbers)


def finish(nc, sem, out, x_perm, ident, ones, wo_sb, bo_sb, node_id, acc):
    with ExitStack() as ps:
        def sb(name, shape, dtype=F32):
            return ps.enter_context(nc.sbuf_tensor(name, shape, dtype))

        def pp(name, shape, dtype=F32):
            return ps.enter_context(nc.psum_tensor(name, shape, dtype))

        x = sb("x", [P, 2, D])
        z = sb("z", [P, 2, HEADS])
        o, oT = sb("o", [P, 2, D]), sb("oT", [P, 2, D])
        y = sb("y", [P, 2, D])
        stats, mv, rstd = sb("stats", [P, 2, 6]), sb("mv", [P, 2, 2]), sb("rstd", [P, 2, 1])
        res = sb("res", [P, 2, D])
        oT_ps = [pp("oT_ps0", [P, 512]), pp("oT_ps1", [P, 512])]
        y_ps = [pp("y_ps0", [P, 512]), pp("y_ps1", [P, 512])]
        x_in, out_done = [sem("x_in0"), sem("x_in1")], [sem("out_done0"), sem("out_done1")]
        zmax, zinv, o_made, oT_made, oT_staged, proj_made, y_made, stats_made, mv_made, std_made, rstd_made, res_made, eps_set = (
            sem(n) for n in ("zmax", "zinv", "o_made", "oT_made", "oT_staged", "proj_made", "y_made", "stats_made",
                             "mv_made", "std_made", "rstd_made", "res_made", "eps_set"))
        eps_sb = sb("eps_sb", [P, 1])

        with nc.Block() as block:
            @block.sync
            def _(sp):
                for h in range(2):
                    sp.dma_start(x[:, h, :], x_perm[h * P:(h + 1) * P, :]).then_inc(x_in[h], 16)
                with sp.Fori(1, TILES // 2) as i:
                    for h in range(2):
                        sp.wait_ge(y_made, 2 * i + h - 1)
                        sp.dma_start(x[:, h, :], x_perm[bass.ds(i * (2 * P) + h * P, P), :]).then_inc(x_in[h], 16)

            @block.vector
            def _(dve):
                def normalise(t, h, first=False):
                    if not first:
                        dve.wait_ge(oT_made, t - 1)
                    a = acc[:, bass.ds(t * VW, VW)].rearrange("p (g w) -> p g w", w=HD + 1)
                    dve.tensor_scalar(z[:, h, :].unsqueeze(2), a[:, :, HD:HD + 1], 1e-30, None, ALU.max).then_inc(zmax, 1)
                    dve.wait_ge(zmax, t + 1)
                    dve.reciprocal(z[:, h, :], z[:, h, :]).then_inc(zinv, 1)
                    dve.wait_ge(zinv, t + 1)
                    dve.tensor_tensor(o[:, h, :].rearrange("p (g w) -> p g w", w=HD), a[:, :, 0:HD],
                                      z[:, h, :].unsqueeze(2).to_broadcast([P, HEADS, HD]), ALU.mult).then_inc(o_made, 1)

                def moments(t, i, h):
                    dve.wait_ge(proj_made, t + 1)
                    dve.wait_ge(x_in[h], 16 * i + 16)
                    dve.tensor_tensor(y[:, h, :], y_ps[h][:, 0:D], x[:, h, :], ALU.add).then_inc(y_made, 1)
                    dve.wait_ge(y_made, t + 1)
                    dve.bn_stats(stats[:, h, :], y[:, h, :]).then_inc(stats_made, 1)
                    dve.wait_ge(eps_set, 1)
                    dve.wait_ge(stats_made, t + 1)
                    dve.bn_aggr(mv[:, h, :], stats[:, h, :]).then_inc(mv_made, 1)

                def norm(t, i, h, first=False):
                    dve.wait_ge(std_made, t + 1)
                    dve.reciprocal(rstd[:, h, :], rstd[:, h, :]).then_inc(rstd_made, 1)
                    dve.wait_ge(rstd_made, t + 1)
                    if not first:
                        dve.wait_ge(out_done[h], 16 * i)
                    dve.tensor_scalar(res[:, h, :], y[:, h, :], mv[:, h, 0:1], rstd[:, h, :], ALU.subtract, ALU.mult).then_inc(res_made, 1)

                dve.memset(eps_sb[:, :], EPS).then_inc(eps_set, 1)
                for h in range(2):
                    normalise(h, h, first=True)
                for h in range(2):
                    normalise(2 + h, h)
                    moments(h, 0, h)
                for h in range(2):
                    norm(h, 0, h, first=True)
                with dve.Fori(1, TILES // 2 - 1) as i:
                    for h in range(2):
                        normalise(2 * i + 2 + h, h)
                        moments(2 * i + h, i, h)
                    for h in range(2):
                        norm(2 * i + h, i, h)
                i = TILES // 2 - 1
                for h in range(2):
                    moments(2 * i + h, i, h)
                for h in range(2):
                    norm(2 * i + h, i, h)

            @block.tensor
            def _(pe):
                def project(i, first=False):
                    for h in range(2):
                        pe.wait_ge(o_made, 2 * i + h + 1)
                        for kc in range(2):
                            last = pe.transpose(oT_ps[h][:, kc * P:(kc + 1) * P], o[:, h, kc * P:(kc + 1) * P], ident[:, :])
                        last.then_inc(oT_made, 1)
                    for h in range(2):
                        pe.wait_ge(oT_staged, 2 * i + h + 1)
                        if not first:
                            pe.wait_ge(y_made, 2 * i + h - 1)
                        for kc in range(2):
                            pe.matmul(y_ps[h][:, 0:D], oT[:, h, kc * P:(kc + 1) * P], wo_sb[:, kc, :], start=kc == 0, stop=False)
                        pe.matmul(y_ps[h][:, 0:D], ones[0:1, :], bo_sb[0:1, :], start=False, stop=True).then_inc(proj_made, 1)

                project(0, first=True)
                with pe.Fori(1, TILES // 2) as i:
                    project(i)

            @block.scalar
            def _(act):
                def turned(i):
                    for h in range(2):
                        act.wait_ge(oT_made, 2 * i + h + 1)
                        act.activation(oT[:, h, :], oT_ps[h][:, 0:D], ACT.Copy).then_inc(oT_staged, 1)

                def deviations(i):
                    for h in range(2):
                        act.wait_ge(mv_made, 2 * i + h + 1)
                        act.activation(rstd[:, h, :], mv[:, h, 1:2], ACT.Sqrt, bias=eps_sb[:, :]).then_inc(std_made, 1)

                act.wait_ge(eps_set, 1)
                turned(0)
                with act.Fori(1, TILES // 2) as i:
                    turned(i)
                    deviations(i - 1)
                deviations(TILES // 2 - 1)

            @block.gpsimd
            def _(pool):
                for t in range(TILES):
                    pool.wait_ge(res_made, t + 1)
                    pool.indirect_dma_start(out=out, out_offset=bass.IndirectOffsetOnAxis(ap=node_id[:, t:t + 1], axis=0),
                                            in_=res[:, t % 2, :], in_offset=None,
                                            bounds_check=N - 1, oob_is_err=False).then_inc(out_done[t % 2], 16)
                for h in range(2):
                    pool.wait_ge(out_done[h], 16 * TILES // 2)




def kernel(x, src, dst, L0_gnn_Wq, L0_gnn_bq, L0_gnn_Wk, L0_gnn_bk, L0_gnn_Wv, L0_gnn_bv, L0_gnn_Wo, L0_gnn_bo):
    import numpy as np
    import concourse.bacc as bacc
    from concourse.bass_utils import run_bass_kernel_spmd

    by_head = np.arange(D).reshape(HD, HEADS).T.reshape(-1)

    def contraction_first(w):
        return np.ascontiguousarray(np.asarray(w).reshape(2, P, -1).transpose(1, 0, 2))

    rows = np.zeros((NP, XW), np.float32)
    rows[:N, :D] = np.asarray(x)
    wq, wk, wv = (np.asarray(w)[by_head].T for w in (L0_gnn_Wq, L0_gnn_Wk, L0_gnn_Wv))
    arrays = {
        "x_rows": rows,
        "xT": contraction_first(rows[:, :D].T),
        "src": np.ascontiguousarray(np.asarray(src).reshape(EP, EF)),
        "dst": np.ascontiguousarray(np.asarray(dst).reshape(EP, EF)),
        "wkvT": contraction_first(np.concatenate([wk, wv], 1)),
        "bkv": np.concatenate([np.asarray(L0_gnn_bk)[by_head], np.asarray(L0_gnn_bv)[by_head]])[None],
        "wqT": contraction_first(wq),
        "bq": np.asarray(L0_gnn_bq)[by_head][None],
        "woT": contraction_first(np.asarray(L0_gnn_Wo)[:, by_head].T),
        "bo": np.asarray(L0_gnn_bo)[None],
    }
    nc = bacc.Bacc("TRN2", target_bir_lowering=False, num_devices=1)
    args = [nc.dram_tensor(f"in_{name}", a.shape, mybir.dt.from_np(a.dtype), kind="ExternalInput").ap() for name, a in arrays.items()]
    out = nc.dram_tensor("out_rows", (N, D), F32, kind="ExternalOutput").ap()
    gnn_kernel(nc, *args, out)
    r = run_bass_kernel_spmd(nc, [{f"in_{name}": a for name, a in arrays.items()}], core_ids=[0])
    return r.results[0]["out_rows"]
```

```python
from contextlib import ExitStack

import concourse.bass as bass
from concourse import mybir

P = 128
N, D, E = 12500, 256, 200000
HEADS = 8
HD = D // HEADS
TILES = (N + P - 1) // P
NP = TILES * P
QW = D + 1
VW = HEADS * (HD + 1)
KVW = D + VW
PW = 3 * D
BW = PW + D
R = 4
EP = 125
EF = E // EP
FBITS, PBITS = 11, 7
SF = 1 << FBITS
HALF, QUARTER = SF // 2, SF // 4
SLOTS = P * SF
ROW_SHIFT = 14
COL_MASK = (1 << ROW_SHIFT) - 1
KEY_BASE = 0x20000000
SENTINEL = KEY_BASE | (COL_MASK << ROW_SHIFT)
CH = 320
CHUNKS = EF // CH
POOL_HOTS = 28
CLIP = 1022
G = 3
QR = 2 * R
BP = 65
C = 48
TAB = TILES + 1
U = 4
LOOPS = (int((E / P + C + TILES * (G - 1)) // G) - 1 + U - 1) // U
STEPS = LOOPS * U + 1
NEG = -3.0e30
M0 = -1.0e30
SCALE = HD ** -0.5
EPS = 1e-5
RUNG = 14
assert TILES % RUNG == 0 and C % G == 0 and EF % CH == 0

F32, I32, BF16 = mybir.dt.float32, mybir.dt.int32, mybir.dt.bfloat16
ALU = mybir.AluOpType
ACT = mybir.ActivationFunctionType
AX = mybir.AxisListType


def prepare(nc, sem, x_rows, xT, src, dst, wT, bias, woT, kv_rows, node_rows, edge_keys, q_perm,
            ident, ones, upper, bias_parts, ones_b, wo_sb, node_id, start_f, tile_deg, gmax_i):
    with ExitStack() as ps:
        def sb(name, shape, dtype=F32):
            return ps.enter_context(nc.sbuf_tensor(name, shape, dtype))

        def pp(name, shape, dtype=F32):
            return ps.enter_context(nc.psum_tensor(name, shape, dtype))

        A = [sb("sort_a", [P, SF]), sb("sort_b", [P, SF])]
        src_sb = sb("src_sb", [EP, EF], I32)
        dst_sb = A[1][0:EP, 0:EF].bitcast(I32)
        hi_b, lo_b = sb("hi_b", [EP, EF], BF16), sb("lo_b", [EP, EF], BF16)
        hot_hi, hot_lo = sb("hot_hi", [EP, TILES, CH], BF16), sb("hot_lo", [EP, P, CH], BF16)
        digit = hot_hi[:, 0:2 * EF // CH, :].rearrange("p v e -> p (v e)").bitcast(I32)
        early_f = hot_lo[0:BP, :, :].rearrange("p v e -> p (v e)")
        bias_f, part = early_f[:, 0:2 * BW].bitcast(F32), early_f[:, 2 * BW:3 * BW]
        w_sb = sb("w_sb", [P, 2, PW])
        xt_sb = sb("xt_sb", [P, R, 2, P])
        kv_st, q_st = sb("kv_st", [P, R, KVW]), sb("q_st", [P, R, D])
        qg = kv_st[:, :, :].rearrange("p r w -> p (r w)").rearrange("p (r w) -> p r w", r=QR)
        pid, gray, sgn_i = sb("pid", [P, 1], I32), sb("gray", [P, 1], I32), sb("sgn_i", [P, 9], I32)
        sgn = sb("sgn", [P, 9])
        O = [sb("ord_a", [P, P]), sb("ord_b", [P, P])]
        nid_f, deg, excl = sb("nid_f", [P, P]), sb("deg", [P, P]), sb("excl", [P, P])
        start_i, ord_i = sb("start_i", [P, P], I32), sb("ord_i", [P, P], I32)
        row_sum, row_max, row_off, gmax_f = (sb(x, [P, 1]) for x in ("row_sum", "row_max", "row_off", "gmax_f"))

        hist_ps, misc_ps = pp("hist_ps", [P, 512]), pp("misc_ps", [P, 512])
        kv_ps = [pp("kv_ps0", [P, 512]), pp("kv_ps1", [P, 512])]
        q_ps = [pp("q_ps0", [P, 512]), pp("q_ps1", [P, 512])]
        T_ps = [pp("T_ps0", [P, QUARTER]), pp("T_ps1", [P, QUARTER])]

        src_in, dst_in, w_in, bias_in, wo_in, consts, digits = (
            sem(x) for x in ("src_in", "dst_in", "w_in", "bias_in", "wo_in", "consts", "digits"))
        hots_made, pool_hots_made, hot_used = sem("hots_made"), sem("pool_hots_made"), sem("hot_used")
        sort_done = sem("sort_done")
        offs_made, ord_turned, nodes_ready = sem("offs_made"), sem("ord_turned"), sem("nodes_ready")
        starts_ready, starts_out = sem("starts_ready"), sem("starts_out")
        xt_in, kv_out, q_out = ([sem(f"{x}{j}") for j in range(R)] for x in ("xt_in", "kv_out", "q_out"))
        kv_made, kv_staged = sem("kv_made"), sem("kv_staged")
        turned, unturned = sem("turned"), sem("unturned")
        qg_in, qg_out = ([sem(f"{x}{j}") for j in range(QR)] for x in ("qg_in", "qg_out"))
        start_taken = sem("start_taken")
        keys_out, idle_out = sem("keys_out"), sem("idle_out")

        SPAN = range(FBITS + 1, FBITS + PBITS + 1)
        HOT_AT = {1: 0, 5: 1, 7: 2, 8: 3, 9: 4}
        ORDER_AT = 10
        BODIES = TILES // R
        EARLY, MIDDLE = [3, 3, 2, 2, 0], 3
        AFTER_TURN = {1: 1, 3: 1, 5: 1, 7: 1, 9: 1, 11: 1}
        AFTER_PHASE = {15: 2, 16: 3}
        assert sum(EARLY) + MIDDLE + sum(AFTER_TURN.values()) + sum(AFTER_PHASE.values()) == BODIES
        at = {}
        order_T = []
        halves = []

        with nc.Block() as block:

            @block.vector
            def _(dve):
                n = [0]

                mine = {"edges": 0, "nodes": 0}

                def did(ins, who="edges"):
                    n[0] += 1
                    mine[who] = n[0]
                    ins.then_inc(sort_done, 1)

                def settle(who="edges"):
                    dve.wait_ge(sort_done, mine[who])

                def stage(bufs, c, lo, width, bit):
                    a, b = (bufs[x][:, lo:lo + width].rearrange("p (m two j) -> p m two j", two=2, j=1 << bit) for x in (c, 1 - c))
                    settle()
                    did(dve.tensor_tensor(b[:, :, 0, :], a[:, :, 0, :], a[:, :, 1, :], ALU.min))
                    beside()
                    did(dve.tensor_tensor(b[:, :, 1, :], a[:, :, 0, :], a[:, :, 1, :], ALU.max))
                    beside()
                    return 1 - c

                def flip(t, by=-1.0):
                    settle()
                    did(dve.tensor_scalar(t, t, by, None, ALU.mult))

                def flip_after(t, width, k):
                    w = (width - 1).bit_length()
                    if k < w - 1:
                        flip(t[:, 0:width].rearrange("p (m w) -> p m w", w=4 << k)[:, :, 1 << k:3 << k])
                    elif k == w - 1:
                        flip(t[:, 0:width // 2], sgn[:, 7:8])
                        flip(t[:, width // 2:width], sgn[:, 8:9])

                def hot_chunk(c):
                    if c:
                        dve.wait_ge(hot_used, c)
                    for v in range(P):
                        dve.tensor_scalar(hot_lo[:, v, :], lo_b[:, c * CH:(c + 1) * CH], float(v), None, ALU.is_equal)
                    for v in range(POOL_HOTS, TILES):
                        last = dve.tensor_scalar(hot_hi[:, v, :], hi_b[:, c * CH:(c + 1) * CH], float(v), None, ALU.is_equal)
                    last.then_inc(hots_made, 1)

                keys = A[0][0:EP, 0:EF].bitcast(I32)
                did(dve.memset(A[0][:, :].bitcast(I32), SENTINEL))
                did(dve.memset(bias_f[:, :], 0.0))
                did(dve.memset(ones_b[:, :], 1.0))
                at["cleared"] = n[0]
                for h in range(R):
                    did(dve.memset(kv_st[:, h, D:KVW].rearrange("p (g w) -> p g w", w=HD + 1)[:, :, HD:HD + 1], 1.0))
                at["ones"] = n[0]
                dve.wait_ge(src_in, 16)
                did(dve.tensor_scalar(digit, src_sb[:, :], PBITS, None, ALU.logical_shift_right))
                settle()
                dve.tensor_copy(hi_b[:, :], digit).then_inc(digits, 1)
                dve.wait_ge(digits, 1)
                did(dve.tensor_scalar(digit, src_sb[:, :], P - 1, None, ALU.bitwise_and))
                settle()
                dve.tensor_copy(lo_b[:, :], digit).then_inc(digits, 1)
                did(dve.tensor_scalar(keys, src_sb[:, :], ROW_SHIFT, KEY_BASE, ALU.logical_shift_left, ALU.bitwise_or))
                dve.wait_ge(dst_in, 16)
                settle()
                did(dve.tensor_tensor(keys, keys, dst_sb, ALU.bitwise_or))
                dve.wait_ge(bias_in, 48)
                did(dve.tensor_copy(bias_parts[:, :], bias_f[:, :]))
                settle()
                did(dve.tensor_tensor(bias_f[:, :], bias_f[:, :], bias_parts[:, :], ALU.subtract))
                settle()
                did(dve.tensor_copy(part[:, :], bias_f[:, :]))
                settle()
                did(dve.tensor_tensor(bias_f[:, :], bias_f[:, :], part[:, :], ALU.subtract))
                did(dve.tensor_copy(bias_parts[32:33, :], part[32:33, :]))
                settle()
                did(dve.tensor_copy(bias_parts[64:65, :], bias_f[64:65, :]))
                at["bias"] = n[0]
                dve.wait_ge(consts, 7)
                did(dve.tensor_scalar(gray[:, :], pid[:, :], 1, None, ALU.logical_shift_right))
                settle()
                did(dve.tensor_tensor(gray[:, :], gray[:, :], pid[:, :], ALU.bitwise_xor))
                settle()
                for a in range(PBITS):
                    did(dve.tensor_scalar(sgn_i[:, a:a + 1], gray[:, :], a, 1, ALU.logical_shift_right, ALU.bitwise_and))
                did(dve.tensor_scalar(sgn_i[:, 7:8], pid[:, :], 1, None, ALU.bitwise_and))
                settle()
                did(dve.tensor_scalar(sgn[:, 0:8], sgn_i[:, 0:8], -2.0, 1.0, ALU.mult, ALU.add))
                settle()
                did(dve.tensor_scalar(sgn[:, 8:9], sgn[:, 7:8], -1.0, None, ALU.mult))
                dve.wait_ge(digits, 2)

                def order_nodes():
                    def did_(ins):
                        did(ins, "nodes")

                    def settle_():
                        settle("nodes")

                    dve.wait_ge(hot_used, CHUNKS)
                    did_(dve.memset(deg[:, :], 0.0))
                    yield
                    settle_()
                    did_(dve.tensor_copy(deg[0:TILES, :], hist_ps[0:TILES, 0:P]))
                    yield
                    settle_()
                    did_(dve.tensor_tensor_scan(excl[:, :], ones[:, :], deg[:, :], 0.0, ALU.mult, ALU.add))
                    did_(dve.tensor_reduce(row_max[:, :], deg[:, :], AX.X, ALU.max))
                    yield
                    settle_()
                    did_(dve.tensor_copy(row_sum[:, :], excl[:, P - 1:P]))
                    at["row_sum"] = n[0]
                    settle_()
                    did_(dve.tensor_tensor(excl[:, :], excl[:, :], deg[:, :], ALU.subtract))
                    did_(dve.tensor_scalar(deg[:, :], deg[:, :], float(CLIP), -1.0, ALU.min, ALU.mult))
                    did_(dve.tensor_scalar(O[1][:, :], nid_f[:, :], float(N), float((CLIP + 1) << ROW_SHIFT), ALU.is_ge, ALU.mult))
                    yield
                    settle_()
                    did_(dve.tensor_scalar(deg[:, :], deg[:, :], float(CLIP), float(1 << ROW_SHIFT), ALU.add, ALU.mult))
                    yield
                    settle_()
                    did_(dve.tensor_tensor(deg[:, :], deg[:, :], O[1][:, :], ALU.max))
                    yield
                    settle_()
                    did_(dve.tensor_tensor(O[0][:, :], deg[:, :], nid_f[:, :], ALU.add))
                    yield
                    dve.wait_ge(offs_made, 1)
                    did_(dve.tensor_copy(row_off[:, :], misc_ps[:, 256:257]))
                    did_(dve.tensor_reduce(gmax_f[0:1, :], misc_ps[0:1, 128:256], AX.X, ALU.max))
                    yield
                    settle_()
                    did_(dve.tensor_copy(gmax_i[:, :], gmax_f[0:1, :]))
                    dve.tensor_scalar(start_i[:, :], excl[:, :], row_off[:, :], None, ALU.add).then_inc(starts_ready, 1)
                    early = O[0][:, :].rearrange("p (m w) -> p m w", w=4)[:, :, 2:4]
                    did_(dve.tensor_scalar(early, early, -1.0, None, ALU.mult))
                    o = 0
                    for k in range(1, 2 * PBITS + 1):
                        for bits, turns in ((range(k - PBITS - 1, -1, -1), True), (range(min(k, PBITS) - 1, -1, -1), False)):
                            if k > PBITS:
                                order_T.append((o, mine["nodes"]))
                                yield
                                yield
                                dve.wait_ge(ord_turned, len(order_T))
                                did_(dve.tensor_copy(O[1 - o][:, :], misc_ps[:, 0:P]))
                                o = 1 - o
                                yield
                            elif turns:
                                continue
                            for bit in bits:
                                a, b = (O[x][:, :].rearrange("p (m two j) -> p m two j", two=2, j=1 << bit) for x in (o, 1 - o))
                                settle_()
                                did_(dve.tensor_tensor(b[:, :, 0, :], a[:, :, 0, :], a[:, :, 1, :], ALU.min))
                                did_(dve.tensor_tensor(b[:, :, 1, :], a[:, :, 0, :], a[:, :, 1, :], ALU.max))
                                o = 1 - o
                                yield
                        settle_()
                        if k < PBITS - 1:
                            part_ = O[o][:, :].rearrange("p (m w) -> p m w", w=4 << k)[:, :, 1 << k:3 << k]
                            did_(dve.tensor_scalar(part_, part_, -1.0, None, ALU.mult))
                        elif k == PBITS - 1:
                            for h in range(2):
                                part_ = O[o][:, h * (P // 2):(h + 1) * (P // 2)]
                                did_(dve.tensor_scalar(part_, part_, sgn[:, 7 + h:8 + h], None, ALU.mult))
                        elif k < 2 * PBITS:
                            did_(dve.tensor_scalar(O[o][:, :], O[o][:, :], sgn[:, k - PBITS:k - PBITS + 1], None, ALU.mult))
                        yield
                    settle_()
                    did_(dve.tensor_copy(sgn_i[:, 8:9], O[o][:, 0:1]))
                    order_T.append((o, mine["nodes"]))
                    yield
                    yield
                    dve.wait_ge(ord_turned, len(order_T))
                    did_(dve.tensor_copy(ord_i[:, :], misc_ps[:, 0:P]))
                    yield
                    settle_()
                    dve.tensor_scalar(node_id[:, :], ord_i[:, :], COL_MASK, None, ALU.bitwise_and).then_inc(nodes_ready, 1)
                    did_(dve.tensor_scalar(sgn_i[:, 8:9], sgn_i[:, 8:9], ROW_SHIFT, None, ALU.logical_shift_right))
                    yield
                    settle_()
                    did_(dve.tensor_copy(tile_deg[:, :], sgn_i[:, 8:9]))
                    yield
                    settle_()
                    did_(dve.tensor_scalar(tile_deg[:, :], tile_deg[:, :], -1.0, float(CLIP), ALU.mult, ALU.add))
                    yield
                    settle_()
                    did_(dve.tensor_scalar(row_max[:, :], tile_deg[:, :], float(CLIP), float(E), ALU.is_ge, ALU.mult))
                    yield
                    settle_()
                    did_(dve.tensor_tensor(tile_deg[:, :], tile_deg[:, :], row_max[:, :], ALU.add))

                ordering = order_nodes()
                begun = [False]

                def beside():
                    if begun[0]:
                        next(ordering, None)

                flip(A[0][:, :].rearrange("p (m w) -> p m w", w=4)[:, :, 2:4])
                c = 0
                for k in range(1, FBITS + 1):
                    if k in HOT_AT:
                        hot_chunk(HOT_AT[k])
                    if k == ORDER_AT:
                        begun[0] = True
                    for bit in range(k - 1, -1, -1):
                        c = stage(A, c, 0, SF, bit)
                    if k < FBITS:
                        flip_after(A[c], SF, k)
                for h in range(2):
                    flip(A[c][:, h * HALF:(h + 1) * HALF], sgn[:, 0:1])
                at[FBITS + 1, "to", 0] = at[FBITS + 1, "to", 1] = n[0]

                for k in SPAN:
                    there = 1 - c
                    for h in range(2):
                        o = there
                        dve.wait_ge(unturned, 8 * (k - SPAN[0]) + 2 * h + 2)
                        for bit in range(k - FBITS - 1, -1, -1):
                            o = stage(A, o, h * HALF, HALF, bit)
                        at[k, "back", h] = n[0]
                    halves.append(((c, there), (o, 1 - o)))
                    c = 1 - o
                    dve.wait_ge(unturned, 8 * (k - SPAN[0]) + 8)
                    c = stage(A, c, 0, SF, FBITS - 1)
                    for h in range(2):
                        o = c
                        for bit in range(FBITS - 2, -1, -1):
                            o = stage(A, o, h * HALF, HALF, bit)
                        if k != SPAN[-1]:
                            flip(A[o][:, h * HALF:(h + 1) * HALF], sgn[:, k - FBITS:k - FBITS + 1])
                            at[k + 1, "to", h] = n[0]
                    c = o
                at["keys"] = (n[0], c)

            work = []
            turns = [(value, "nodes", i) for i, (o, value) in enumerate(order_T)]
            quarters = [(at[k, way, r // 2], "quarter", (k, way, r)) for k in SPAN for way in ("to", "back") for r in range(4)]
            done = sum(EARLY) + MIDDLE
            for value, what, which in sorted(turns + quarters, key=lambda ask: ask[0]):
                work.append((what, which))
                more = AFTER_TURN.get(which, 0) if what == "nodes" else AFTER_PHASE.get(which[0], 0) if which[1:] == ("back", 3) else 0
                if more:
                    work.append(("bodies", (done, done + more)))
                    done += more
                    if done == BODIES:
                        work.append(("tiles", range(BODIES * R, TILES)))

            @block.sync
            def _(sp):
                sp.dma_start(src_sb[:, :], src).then_inc(src_in, 16)
                sp.dma_start(dst_sb, dst).then_inc(dst_in, 16)
                sp.dma_start(w_sb[:, :, :], wT).then_inc(w_in, 16)
                sp.wait_ge(sort_done, at["cleared"])
                for p in (0, 32, 64):
                    sp.dma_start(bias_f[p:p + 1, :], bias).then_inc(bias_in, 16)
                sp.dma_start(wo_sb[:, :, :], woT).then_inc(wo_in, 16)
                sp.dma_start(q_perm[NP:NP + P, :], x_rows[0:P, :]).then_inc(idle_out, 16)

                def load_x(t, j):
                    sp.dma_start(xt_sb[:, j, :, :], xT[:, :, bass.ds(t * P, P)]).then_inc(xt_in[j], 16)

                def store_rows(t, j):
                    sp.wait_ge(kv_staged, t + 1)
                    sp.dma_start(kv_rows[bass.ds(t * P, P), :], kv_st[:, j, :]).then_inc(kv_out[j], 16)
                    sp.dma_start(node_rows[bass.ds(t * P, P), 0:D], q_st[:, j, :]).then_inc(q_out[j], 16)

                for j in range(R):
                    load_x(j, j)
                with sp.Fori(0, BODIES - 1) as i:
                    for j in range(R):
                        sp.wait_ge(kv_made, i * R + j + 1)
                        load_x(i * R + j + R, j)
                        store_rows(i * R + j, j)
                for t in range(BODIES * R - R, TILES):
                    if t + R < TILES:
                        sp.wait_ge(kv_made, t + 1)
                        load_x(t + R, t % R)
                    store_rows(t, t % R)
                sp.wait_ge(starts_ready, 1)
                sp.dma_start(node_rows[:, D:D + 1].rearrange("(p f) one -> p (f one)", f=P),
                             start_i[0:TILES, :].bitcast(F32), allow_slow_non_contiguous=True).then_inc(starts_out, 16)

                def store_q(t, j, turn):
                    sp.wait_ge(qg_in[j], 16 * turn + 16)
                    sp.dma_start(q_perm[bass.ds(t * P, P), :], qg[:, j, 0:D]).then_inc(qg_out[j], 16)

                with sp.Fori(0, TILES // QR) as i:
                    for j in range(QR):
                        store_q(i * QR + j, j, i)
                for t in range(TILES // QR * QR, TILES):
                    store_q(t, t % QR, TILES // QR)
                sp.wait_ge(sort_done, at["keys"][0])
                sp.dma_start(edge_keys.rearrange("(p f) one -> p (f one)", f=SF), A[at["keys"][1]][:, :].bitcast(I32)).then_inc(keys_out, 16)
                sp.wait_ge(wo_in, 16)
                sp.wait_ge(idle_out, 16)
                sp.wait_ge(keys_out, 16)
                for j in range(R):
                    sp.wait_ge(kv_out[j], 16 * len(range(j, TILES, R)))
                    sp.wait_ge(q_out[j], 16 * len(range(j, TILES, R)))
                for j in range(QR):
                    sp.wait_ge(qg_out[j], 16 * len(range(j, TILES, QR)))

            @block.gpsimd
            def _(pool):
                pool.memset(ident[:, :], 0.0).then_inc(consts, 1)
                pool.memset(upper[:, :], 1.0).then_inc(consts, 1)
                pool.memset(ones[:, :], 1.0).then_inc(consts, 1)
                pool.wait_ge(consts, 3)
                pool.affine_select(out=ident[:, :], in_=ident[:, :], compare_op=ALU.not_equal, fill=1.0, base=0,
                                   pattern=[[-1, P]], channel_multiplier=1).then_inc(consts, 1)
                pool.affine_select(out=upper[:, :], in_=upper[:, :], compare_op=ALU.is_gt, fill=0.0, base=0,
                                   pattern=[[1, P]], channel_multiplier=-1).then_inc(consts, 1)
                pool.iota(pid[:, :], pattern=[[0, 1]], base=0, channel_multiplier=1).then_inc(consts, 1)
                pool.iota(nid_f[:, :], pattern=[[1, P]], base=0, channel_multiplier=P,
                          allow_small_or_imprecise_dtypes=True).then_inc(consts, 1)
                pool.wait_ge(digits, 2)
                for c in range(CHUNKS):
                    if c:
                        pool.wait_ge(hot_used, c)
                    for v in range(POOL_HOTS):
                        last = pool.tensor_scalar(hot_hi[:, v, :], hi_b[:, c * CH:(c + 1) * CH], float(v), None, ALU.is_equal)
                    last.then_inc(pool_hots_made, 1)
                pool.wait_ge(nodes_ready, 1)
                for j in range(R):
                    pool.wait_ge(q_out[j], 16 * len(range(j, TILES, R)))
                    pool.wait_ge(kv_out[j], 16 * len(range(j, TILES, R)))
                pool.wait_ge(starts_out, 16)
                for t in range(TILES):
                    if t >= QR:
                        pool.wait_ge(qg_out[t % QR], 16 * (t // QR))
                        pool.wait_ge(start_taken, t - QR + 1)
                    pool.indirect_dma_start(out=qg[:, t % QR, 0:QW], out_offset=None, in_=node_rows,
                                            in_offset=bass.IndirectOffsetOnAxis(ap=node_id[:, t:t + 1], axis=0),
                                            bounds_check=NP - 1, oob_is_err=False).then_inc(qg_in[t % QR], 16)

            @block.tensor
            def _(pe):
                def count_chunk(c):
                    pe.wait_ge(hots_made, c + 1)
                    pe.wait_ge(pool_hots_made, c + 1)
                    for e in range(CH):
                        last = pe.matmul(hist_ps[0:TILES, 0:P], hot_hi[:, :, e], hot_lo[:, :, e],
                                         start=c == 0 and e == 0, stop=c == CHUNKS - 1 and e == CH - 1)
                    last.then_inc(hot_used, 1)

                def project(t, j, turn, first=False):
                    pe.wait_ge(xt_in[j], 16 * turn + 16)
                    if not first:
                        pe.wait_ge(kv_staged, t - 1)
                    for ps, a, b in ((kv_ps[j % 2], 0, 2 * D), (q_ps[j % 2], 2 * D, PW)):
                        for kc in range(2):
                            pe.matmul(ps[:, 0:b - a], xt_sb[:, j, kc, :], w_sb[:, kc, a:b], start=kc == 0, stop=False)
                        last = pe.matmul(ps[:, 0:b - a], ones_b[:, :], bias_parts[:, a:b], start=False, stop=True)
                    last.then_inc(kv_made, 1)

                def project_bodies(a, b):
                    if a == 0:
                        for j in range(R):
                            project(j, j, 0, first=j < 2)
                    if b > max(a, 1):
                        with pe.Fori(max(a, 1), b) as i:
                            for j in range(R):
                                project(i * R + j, j, i)

                pe.wait_ge(consts, 7)
                done = 0
                for c in range(CHUNKS):
                    count_chunk(c)
                    if c == 0:
                        pe.wait_ge(w_in, 16)
                        pe.wait_ge(sort_done, at["bias"])
                    project_bodies(done, done + EARLY[c])
                    done += EARLY[c]
                pe.wait_ge(sort_done, at["row_sum"])
                pe.matmul(misc_ps[:, 256:257], upper[:, :], row_sum[:, :], start=True, stop=True)
                pe.matmul(misc_ps[0:1, 128:256], row_max[:, :], ident[:, :], start=True, stop=True).then_inc(offs_made, 1)
                project_bodies(done, done + MIDDLE)
                def turn_quarter(k, way, r):
                    count = 8 * (k - SPAN[0]) + 4 * (way == "back") + r
                    pe.wait_ge(sort_done, at[k, way, r // 2])
                    if count >= 2:
                        pe.wait_ge(unturned, count - 1)
                    a = A[halves[k - SPAN[0]][way == "back"][0]]
                    for b in range(QUARTER // P):
                        last = pe.transpose(T_ps[r % 2][:, b * P:(b + 1) * P],
                                            a[:, r * QUARTER + b * P:r * QUARTER + (b + 1) * P], ident[:, :])
                    last.then_inc(turned, 1)

                for what, which in work:
                    if what == "nodes":
                        pe.wait_ge(sort_done, order_T[which][1])
                        pe.transpose(misc_ps[:, 0:P], O[order_T[which][0]][:, :], ident[:, :]).then_inc(ord_turned, 1)
                    elif what == "quarter":
                        turn_quarter(*which)
                    elif what == "bodies":
                        project_bodies(*which)
                    else:
                        for t in which:
                            project(t, t % R, BODIES)

            @block.scalar
            def _(act):
                def stage_rows(t, j, turn, first=False):
                    act.wait_ge(kv_made, t + 1)
                    if not first:
                        act.wait_ge(kv_out[j], 16 * turn)
                        act.wait_ge(q_out[j], 16 * turn)
                    act.activation(kv_st[:, j, 0:D], kv_ps[j % 2][:, 0:D], ACT.Copy)
                    act.activation(kv_st[:, j, D:KVW].rearrange("p (g w) -> p g w", w=HD + 1)[:, :, 0:HD],
                                   kv_ps[j % 2][:, D:2 * D].rearrange("p (g w) -> p g w", w=HD), ACT.Copy)
                    act.activation(q_st[:, j, :], q_ps[j % 2][:, 0:D], ACT.Copy, scale=SCALE).then_inc(kv_staged, 1)

                def stage_bodies(a, b):
                    if a == 0:
                        for j in range(R):
                            stage_rows(j, j, 0, first=True)
                    if b > max(a, 1):
                        with act.Fori(max(a, 1), b) as i:
                            for j in range(R):
                                stage_rows(i * R + j, j, i)

                act.wait_ge(sort_done, at["ones"])
                stage_bodies(0, sum(EARLY) + MIDDLE)

                def unturn_quarter(k, way, r):
                    act.wait_ge(turned, 8 * (k - SPAN[0]) + 4 * (way == "back") + r + 1)
                    b = A[halves[k - SPAN[0]][way == "back"][1]]
                    act.activation(b[:, r * QUARTER:(r + 1) * QUARTER], T_ps[r % 2][:, :], ACT.Copy).then_inc(unturned, 1)

                for what, which in work:
                    if what == "quarter":
                        unturn_quarter(*which)
                    elif what == "bodies":
                        stage_bodies(*which)
                    elif what == "tiles":
                        for t in which:
                            stage_rows(t, t % R, BODIES)

                def take_start(t, j, turn):
                    act.wait_ge(qg_in[j], 16 * turn + 16)
                    act.activation(start_f[:, bass.ds(t, 1)], qg[:, j, D:QW].bitcast(I32), ACT.Copy).then_inc(start_taken, 1)

                with act.Fori(0, TILES // QR) as i:
                    for j in range(QR):
                        take_start(i * QR + j, j, i)
                for t in range(TILES // QR * QR, TILES):
                    take_start(t, t % QR, TILES // QR)


def bounded(eng, value, most):
    return eng.snap(value).with_bounds(min_val=0, max_val=most)


def gnn_kernel(nc, x_rows, xT, src, dst, wT, bias, woT, out):
    with ExitStack() as ctx:
        def sb(name, shape, dtype=F32):
            return ctx.enter_context(nc.sbuf_tensor(name, shape, dtype))

        def sem(name):
            return ctx.enter_context(nc.semaphore(name))

        kv_rows = nc.dram_tensor("kv_rows", (NP, KVW), F32).ap()
        node_rows = nc.dram_tensor("node_rows", (NP, QW), F32).ap()
        edge_keys = nc.dram_tensor("edge_keys", (SLOTS, 1), I32).ap()
        q_perm = nc.dram_tensor("q_perm", (TAB * P, D), F32).ap()

        ident, ones, upper = sb("ident", [P, P]), sb("ones", [P, P]), sb("upper", [P, P])
        wo_sb = sb("wo_sb", [P, 2, D])
        bias_parts, ones_b = sb("bias_parts", [BP, BW], BF16), sb("ones_b", [BP, P], BF16)
        node_id = sb("node_id", [P, P], I32)
        start_f = sb("start_f", [P, TILES])
        tile_deg = sb("tile_deg", [P, 1])
        gmax_i = sb("gmax_i", [1, 1], I32)

        prepare(nc, sem, x_rows, xT, src, dst, wT, bias, woT, kv_rows, node_rows, edge_keys, q_perm,
                ident, ones, upper, bias_parts, ones_b, wo_sb, node_id, start_f, tile_deg, gmax_i)

        acc = sb("acc", [P, TAB * VW])
        runmax = sb("runmax", [P, TAB * HEADS])
        cols, mask = sb("cols", [P, TAB, C], I32), sb("mask", [P, TAB, C])
        step_tab = sb("step_tab", [1, STEPS + 1], I32)
        round_base = sb("round_base", [P, 1])

        acc_zeroed = sem("acc_zeroed")
        with nc.Block() as block:
            @block.vector
            def _(dve):
                dve.memset(acc[:, 0:TAB * VW // 2], 0.0)
                dve.memset(runmax[:, :], M0)
                dve.memset(round_base[:, :], 0.0)
                dve.memset(mask[:, TILES, :], NEG)
                dve.memset(cols[:, TILES, :], 0).then_inc(acc_zeroed, 1)

            @block.gpsimd
            def _(pool):
                pool.memset(acc[:, TAB * VW // 2:TAB * VW], 0.0).then_inc(acc_zeroed, 1)

        gmax = nc.values_load(gmax_i[0:1, 0:1], min_val=1, max_val=E)
        with nc.Fori(0, (gmax + (C - 1)) // C):
            one_round(nc, sem, kv_rows, edge_keys, q_perm, ident, ones, upper, node_id, start_f, tile_deg,
                      acc, runmax, cols, mask, step_tab, round_base)
        finish(nc, sem, out, x_rows, ident, bias_parts, ones_b, wo_sb, node_id, acc)


def one_round(nc, new_sem, kv_rows, edge_keys, q_perm, ident, ones, upper, node_id, start_f, tile_deg,
              acc, runmax, cols, mask, step_tab, round_base):
    used = []

    def sem(name):
        used.append(new_sem(name))
        return used[-1]

    with ExitStack() as ps:
        def sb(name, shape, dtype=F32):
            return ps.enter_context(nc.sbuf_tensor(name, shape, dtype))

        def pp(name, shape, dtype=F32):
            return ps.enter_context(nc.psum_tensor(name, shape, dtype))

        run_at = sb("run_at", [P, TILES], I32)
        rows = sb("rows", [P, RUNG, C], I32)
        rem, nsteps, ends = sb("rem", [P, 1]), sb("nsteps", [P, 1]), sb("ends", [P, 1])
        thresh = sb("thresh", [P, C // G])
        step_f = sb("step_f", [P, STEPS])
        past = sb("past", [P, STEPS])
        tile_tab = sb("tile_tab", [1, STEPS], I32)
        tile_f, place_f = sb("tile_f", [1, STEPS]), sb("place_f", [1, STEPS])
        idx = sb("idx", [P, U, G], I32)
        kv = sb("kv", [P, U, G, KVW])
        q = sb("q", [P, U, D])
        prod = sb("prod", [P, G, D])
        s = sb("s", [P, 2, (G + 1) * HEADS])
        pv = sb("pv", [P, 2, (G + 1) * VW])
        tab_ps = [pp("tab_ps0", [1, 512]), pp("tab_ps1", [1, 512]), pp("tab_ps2", [1, 512]), pp("tab_ps3", [1, 512])]
        end_ps = pp("end_ps", [P, 512])
        sum_ps = [pp("sum_ps0", [P, 512]), pp("sum_ps1", [P, 512])]

        plan = sem("plan")
        iotas, ends_made, counts_made, tab_ready = sem("iotas"), sem("ends_made"), sem("counts_made"), sem("tab_ready")
        runs_in = [sem(f"runs_in{i}") for i in range(TILES // RUNG)]
        run_at_ready, runs_ready = sem("run_at_ready"), sem("runs_ready")
        idx_ready, kv_in, q_in = sem("idx_ready"), [sem(f"kv_in{j}") for j in range(U)], [sem(f"q_in{j}") for j in range(U)]
        prod_made, scored, old_copied, masked, max_made, diffs_made = (
            sem(x) for x in ("prod_made", "scored", "old_copied", "masked", "max_made", "diffs_made"))
        exp_made, pv_made, carry_made, summed, acc_stored = (
            sem(x) for x in ("exp_made", "pv_made", "carry_made", "summed", "acc_stored"))
        CUT = 512
        pieces = [(a, min(a + CUT, STEPS)) for a in range(0, STEPS, CUT)]
        at = {}

        with nc.Block() as block:

            @block.vector
            def _(dve):
                n = [0]

                def did(ins):
                    n[0] += 1
                    ins.then_inc(plan, 1)

                def settle():
                    dve.wait_ge(plan, n[0])

                did(dve.tensor_scalar(rem[:, :], round_base[:, :], -1.0, None, ALU.mult))
                dve.tensor_scalar(run_at[:, :], start_f[:, :], round_base[:, :], float(SLOTS - C), ALU.add, ALU.min).then_inc(run_at_ready, 1)
                settle()
                did(dve.tensor_scalar(rem[:, :], tile_deg[:, :], rem[:, :], float(C), ALU.add, ALU.min))
                dve.wait_ge(iotas, 2)
                settle()
                did(dve.tensor_scalar(thresh[:, :], thresh[:, :], rem[:, :], None, ALU.is_lt))
                settle()
                did(dve.tensor_reduce(nsteps[:, :], thresh[:, :], AX.X, ALU.add))
                at["nsteps"] = n[0] 
                dve.wait_ge(ends_made, 1)
                did(dve.tensor_copy(ends[:, :], end_ps[:, 0:1]))
                settle()
                did(dve.tensor_scalar(past[:, :], step_f[:, :], ends[:, :], None, ALU.is_ge))
                at["past"] = n[0]
                dve.wait_ge(counts_made, 1)
                for j, (a, b) in enumerate(pieces):
                    did(dve.tensor_copy(tile_f[:, a:b], tab_ps[2 * j][:, 0:b - a]))
                    did(dve.tensor_tensor(place_f[:, a:b], step_f[0:1, a:b], tab_ps[2 * j + 1][:, 0:b - a], ALU.subtract))
                settle()
                did(dve.tensor_copy(tile_tab[:, :], tile_f[:, :]))
                did(dve.tensor_scalar(place_f[:, :], place_f[:, :], float(G), float(C - G), ALU.mult, ALU.min))
                settle()
                did(dve.scalar_tensor_tensor(place_f[:, :], tile_f[:, :], float(C), place_f[:, :], ALU.mult, ALU.add))
                settle()
                did(dve.scalar_tensor_tensor(place_f[:, :], place_f[:, :], float(P), tile_f[:, :], ALU.mult, ALU.add))
                settle()
                did(dve.memset(step_tab[:, STEPS:], TILES))
                settle()
                dve.tensor_copy(step_tab[:, 0:STEPS], place_f[:, :]).then_inc(tab_ready, 1)

                for r in range(TILES // RUNG):
                    dve.wait_ge(runs_in[r], 16 * RUNG)
                    part = cols[:, r * RUNG:(r + 1) * RUNG, :]
                    mpart = mask[:, r * RUNG:(r + 1) * RUNG, :]
                    did(dve.tensor_scalar(rows[:, :, :], part, ROW_SHIFT, COL_MASK, ALU.logical_shift_right, ALU.bitwise_and))
                    did(dve.tensor_scalar(part, part, COL_MASK, None, ALU.bitwise_and))
                    settle()
                    did(dve.tensor_tensor(mpart, rows[:, :, :],
                                          node_id[:, r * RUNG:(r + 1) * RUNG].unsqueeze(2).to_broadcast([P, RUNG, C]), ALU.not_equal))
                    settle()
                    did(dve.tensor_scalar(mpart, mpart, NEG, None, ALU.mult))
                settle()
                dve.tensor_scalar(round_base[:, :], round_base[:, :], float(C), None, ALU.add).then_inc(runs_ready, 1)

                mflat = mask[:, :, :].rearrange("p t c -> p (t c)")

                def score(k, j, b):
                    dve.wait_ge(kv_in[j], 16 * G * (k // U) + 16 * G)
                    dve.wait_ge(q_in[j], 16 * (k // U) + 16)
                    dve.tensor_tensor(prod[:, :, :], kv[:, j, :, 0:D], q[:, j, :].unsqueeze(1).to_broadcast([P, G, D]),
                                      ALU.mult).then_inc(prod_made, 1)

                def score_sum(k, b):
                    dve.wait_ge(prod_made, k + 1)
                    dve.tensor_reduce(s[:, b, 0:G * HEADS], prod[:, :, :].rearrange("p g (h d) -> p (g h) d", d=HD),
                                      AX.X, ALU.add).then_inc(scored, 1)

                def maxima(k, b, col, tile, first=False):
                    if not first:
                        dve.wait_ge(max_made, k)
                    m = runmax[:, bass.ds(tile * HEADS, HEADS)]
                    dve.tensor_copy(s[:, b, G * HEADS:], m).then_inc(old_copied, 1)
                    dve.wait_ge(scored, k + 1)
                    sv = s[:, b, 0:G * HEADS].rearrange("p (g h) -> p g h", h=HEADS)
                    dve.tensor_tensor(sv, sv, mflat[:, bass.ds(col, G)].unsqueeze(2).to_broadcast([P, G, HEADS]), ALU.add).then_inc(masked, 1)
                    dve.wait_ge(tab_ready, 1)
                    dve.wait_ge(masked, k + 1)
                    dve.wait_ge(old_copied, k + 1)
                    dve.tensor_reduce(m, s[:, b, :].rearrange("p (g h) -> p h g", h=HEADS), AX.X, ALU.max).then_inc(max_made, 1)
                    dve.wait_ge(max_made, k + 1)
                    sa = s[:, b, :].rearrange("p (g h) -> p g h", h=HEADS)
                    dve.tensor_tensor(sa, sa, m.unsqueeze(1).to_broadcast([P, G + 1, HEADS]), ALU.subtract).then_inc(diffs_made, 1)

                def weigh(k, j, b, peeled=False):
                    dve.wait_ge(exp_made, k + 1)
                    if not peeled:
                        dve.wait_ge(summed, k - 1)
                    dve.tensor_tensor(pv[:, b, 0:G * VW].rearrange("p (g h w) -> p g h w", g=G, w=HD + 1),
                                      kv[:, j, :, D:KVW].rearrange("p g (h w) -> p g h w", w=HD + 1),
                                      s[:, b, 0:G * HEADS].rearrange("p (g h) -> p g h", h=HEADS).unsqueeze(3).to_broadcast([P, G, HEADS, HD + 1]),
                                      ALU.mult).then_inc(pv_made, 1)

                def carry(k, b, tile, first=False):
                    if not first:
                        dve.wait_ge(acc_stored, k)
                    dve.tensor_tensor(pv[:, b, G * VW:].rearrange("p (h w) -> p h w", w=HD + 1),
                                      acc[:, bass.ds(tile * VW, VW)].rearrange("p (h w) -> p h w", w=HD + 1),
                                      s[:, b, G * HEADS:].unsqueeze(2).to_broadcast([P, HEADS, HD + 1]), ALU.mult).then_inc(carry_made, 1)

                dve.wait_ge(tab_ready, 1)
                dve.wait_ge(runs_ready, 1)
                tile_r = [dve.alloc_register(f"tile_{b}") for b in range(2)]
                col_r = [dve.alloc_register(f"col_{b}") for b in range(2)]

                def look_up(k, b):
                    v = dve.value_load(step_tab[0:1, bass.ds(k, 1)], min_val=0, max_val=TAB * C * P - 1)
                    dve.reg_mov(tile_r[b], v & (P - 1))
                    dve.reg_mov(col_r[b], v >> PBITS)

                def step(k, j, peel=False):
                    j1, b, b1 = (j + 1) % U, j % 2, (j + 1) % 2
                    score(k + 1, j1, b1)
                    weigh(k, j, b, peeled=peel and j < 2)
                    score_sum(k + 1, b1)
                    carry(k, b, bounded(dve, tile_r[b], TILES), first=peel and j == 0)
                    look_up(k + 2, b)
                    maxima(k + 1, b1, bounded(dve, col_r[b1], TAB * C - G), bounded(dve, tile_r[b1], TILES))

                look_up(0, 0)
                look_up(1, 1)
                score(0, 0, 0)
                score_sum(0, 0)
                maxima(0, 0, bounded(dve, col_r[0], TAB * C - G), bounded(dve, tile_r[0], TILES), first=True)
                for j in range(U):
                    step(j, j, peel=True)
                with dve.Fori(1, LOOPS) as kk:
                    for j in range(U):
                        step(kk * U + j, j)
                weigh(STEPS - 1, (STEPS - 1) % U, (STEPS - 1) % 2)
                carry(STEPS - 1, (STEPS - 1) % 2, bounded(dve, tile_r[(STEPS - 1) % 2], TILES))
                for r in tile_r + col_r:
                    dve.free_register(r)

            @block.gpsimd
            def _(pool):
                pool.iota(thresh[:, :], pattern=[[G, C // G]], base=0, channel_multiplier=0,
                          allow_small_or_imprecise_dtypes=True).then_inc(iotas, 1)
                pool.iota(step_f[:, :], pattern=[[1, STEPS]], base=0, channel_multiplier=0,
                          allow_small_or_imprecise_dtypes=True).then_inc(iotas, 1)
                pool.wait_ge(run_at_ready, 1)
                for i in range(TILES):
                    pool.indirect_dma_start(out=cols[:, i, :], out_offset=None, in_=edge_keys,
                                            in_offset=bass.IndirectOffsetOnAxis(ap=run_at[:, i:i + 1], axis=0),
                                            bounds_check=SLOTS - 1, oob_is_err=False).then_inc(runs_in[i // RUNG], 16)


                freed = pool.alloc_register("freed")
                pool.reg_mov(freed, 1)

                def gather(k, j, first=False):
                    pool.wait_ge(idx_ready, k + 1)
                    if not first:
                        pool.wait_ge(pv_made, freed)
                        pool.reg_add(freed, freed, 1)
                    for g in range(G):
                        pool.indirect_dma_start(out=kv[:, j, g, :], out_offset=None, in_=kv_rows,
                                                in_offset=bass.IndirectOffsetOnAxis(ap=idx[:, j, g:g + 1], axis=0),
                                                bounds_check=NP - 1, oob_is_err=False).then_inc(kv_in[j], 16)

                for j in range(U):
                    gather(j, j, first=True)
                with pool.Fori(1, LOOPS) as kk:
                    for j in range(U):
                        gather(kk * U + j, j)
                gather(STEPS - 1, (STEPS - 1) % U)
                pool.free_register(freed)

            @block.sync
            def _(sp):
                def load_q(k, j, first=False):
                    tile = sp.value_load(tile_tab[0:1, bass.ds(k, 1)], min_val=0, max_val=TILES)
                    if not first:
                        sp.wait_ge(prod_made, k - U + 1)
                    sp.dma_start(q[:, j, :], q_perm[bass.ds(tile * P, P), :]).then_inc(q_in[j], 16)

                sp.wait_ge(tab_ready, 1)
                for j in range(U):
                    load_q(j, j, first=True)
                with sp.Fori(1, LOOPS) as kk:
                    for j in range(U):
                        load_q(kk * U + j, j)
                load_q(STEPS - 1, (STEPS - 1) % U)

            @block.scalar
            def _(act):
                cflat = cols[:, :, :].rearrange("p t c -> p (t c)")

                def indices(k, j, first=False):
                    v = act.value_load(step_tab[0:1, bass.ds(k, 1)], min_val=0, max_val=TAB * C * P - 1)
                    col = bounded(act, v >> PBITS, TAB * C - G)
                    if not first:
                        act.wait_ge(kv_in[j], 16 * G * (k // U))
                    act.activation(idx[:, j, :], cflat[:, bass.ds(col, G)], ACT.Copy).then_inc(idx_ready, 1)

                def weights(k, b):
                    act.wait_ge(diffs_made, k + 1)
                    act.activation(s[:, b, :], s[:, b, :], ACT.Exp).then_inc(exp_made, 1)

                def store(k, b):
                    v = act.value_load(step_tab[0:1, bass.ds(k, 1)], min_val=0, max_val=TAB * C * P - 1)
                    tile = bounded(act, v & (P - 1), TILES)
                    act.wait_ge(summed, k + 1)
                    act.activation(acc[:, bass.ds(tile * VW, VW)], sum_ps[b][:, 0:VW], ACT.Copy).then_inc(acc_stored, 1)

                act.wait_ge(tab_ready, 1)
                act.wait_ge(runs_ready, 1)
                for j in range(U):
                    indices(j, j, first=True)
                weights(0, 0)
                with act.Fori(0, LOOPS - 1) as kk:
                    for j in range(U):
                        indices(kk * U + j + U, j)
                        weights(kk * U + j + 1, (j + 1) % 2)
                        store(kk * U + j, j % 2)
                indices(STEPS - 1, (STEPS - 1) % U)
                for j in range(U):
                    k = (LOOPS - 1) * U + j
                    weights(k + 1, (j + 1) % 2)
                    store(k, j % 2)
                store(STEPS - 1, (STEPS - 1) % 2)

            @block.tensor
            def _(pe):
                pe.wait_ge(plan, at["nsteps"])
                pe.matmul(end_ps[:, 0:1], upper[:, :], nsteps[:, :], start=True, stop=False)
                pe.matmul(end_ps[:, 0:1], ident[:, :], nsteps[:, :], start=False, stop=True).then_inc(ends_made, 1)
                pe.wait_ge(plan, at["past"])
                for j, (a, b) in enumerate(pieces):
                    pe.matmul(tab_ps[2 * j][:, 0:b - a], ones[0:TILES, 0:1], past[0:TILES, a:b], start=True, stop=True)
                    last = pe.matmul(tab_ps[2 * j + 1][:, 0:b - a], nsteps[0:TILES, :], past[0:TILES, a:b], start=True, stop=True)
                last.then_inc(counts_made, 1)

                def total(k, b):
                    pe.wait_ge(pv_made, k + 1)
                    for g in range(G):
                        pe.matmul(sum_ps[b][:, 0:VW], ident[:, :], pv[:, b, g * VW:(g + 1) * VW], start=g == 0, stop=False)
                    pe.wait_ge(carry_made, k + 1)
                    pe.matmul(sum_ps[b][:, 0:VW], ident[:, :], pv[:, b, G * VW:], start=False, stop=True).then_inc(summed, 1)

                with pe.Fori(0, LOOPS) as kk:
                    for j in range(U):
                        total(kk * U + j, j % 2)
                total(STEPS - 1, (STEPS - 1) % 2)

        with nc.Block() as block:

            @block.gpsimd
            def _(pool):
                numbers = range(used[0].num, used[-1].num + 1)
                assert len(numbers) == len(used)
                pool.dma_reset(numbers)
                pool.sem_clear(numbers)


def finish(nc, sem, out, x_rows, ident, bias_parts, ones_b, wo_sb, node_id, acc):
    with ExitStack() as ps:
        def sb(name, shape, dtype=F32):
            return ps.enter_context(nc.sbuf_tensor(name, shape, dtype))

        def pp(name, shape, dtype=F32):
            return ps.enter_context(nc.psum_tensor(name, shape, dtype))

        x = sb("x", [P, 2, D])
        z = sb("z", [P, 2, HEADS])
        o, oT = sb("o", [P, 2, D]), sb("oT", [P, 2, D])
        y = sb("y", [P, 2, D])
        stats, mv, rstd = sb("stats", [P, 2, 6]), sb("mv", [P, 2, 2]), sb("rstd", [P, 2, 1])
        res = sb("res", [P, 2, D])
        oT_ps = [pp("oT_ps0", [P, 512]), pp("oT_ps1", [P, 512])]
        y_ps = [pp("y_ps0", [P, 512]), pp("y_ps1", [P, 512])]
        x_in, out_done = [sem("x_in0"), sem("x_in1")], [sem("out_done0"), sem("out_done1")]
        zmax, zinv, o_made, oT_made, oT_staged, proj_made, y_made, stats_made, mv_made, std_made, rstd_made, res_made, eps_set = (
            sem(n) for n in ("zmax", "zinv", "o_made", "oT_made", "oT_staged", "proj_made", "y_made", "stats_made",
                             "mv_made", "std_made", "rstd_made", "res_made", "eps_set"))
        eps_sb = sb("eps_sb", [P, 1])

        with nc.Block() as block:
            @block.vector
            def _(dve):
                def at_tile(t, h, i=None, start=True, turn=True, this=True, last=True):
                    h1 = 1 - h
                    a = acc[:, bass.ds((t + 2) * VW, VW)].rearrange("p (g w) -> p g w", w=HD + 1) if start else None
                    if start:
                        dve.tensor_scalar(z[:, h, :].unsqueeze(2), a[:, :, HD:HD + 1], 1e-30, None, ALU.max).then_inc(zmax, 1)
                    if last:
                        dve.wait_ge(std_made, t)
                        dve.reciprocal(rstd[:, h1, :], rstd[:, h1, :]).then_inc(rstd_made, 1)
                    if start:
                        dve.wait_ge(zmax, t + 3)
                        dve.reciprocal(z[:, h, :], z[:, h, :]).then_inc(zinv, 1)
                    if turn:
                        dve.wait_ge(oT_made, t + 2)
                        dve.tensor_copy(oT[:, h1, :], oT_ps[h1][:, 0:D]).then_inc(oT_staged, 1)
                    if start:
                        dve.wait_ge(zinv, t + 3)
                        dve.tensor_tensor(o[:, h, :].rearrange("p (g w) -> p g w", w=HD), a[:, :, 0:HD],
                                          z[:, h, :].unsqueeze(2).to_broadcast([P, HEADS, HD]), ALU.mult).then_inc(o_made, 1)
                    if this:
                        dve.wait_ge(proj_made, t + 1)
                        dve.wait_ge(x_in[h], 16 * i + 16)
                        dve.tensor_tensor(y[:, h, :], y_ps[h][:, 0:D], x[:, h, :], ALU.add).then_inc(y_made, 1)
                        dve.wait_ge(y_made, t + 1)
                        dve.bn_stats(stats[:, h, :], y[:, h, :]).then_inc(stats_made, 1)
                    if last:
                        dve.wait_ge(rstd_made, t)
                        if not (isinstance(t, int) and t < 3):
                            dve.wait_ge(out_done[h1], 16 * (i if h else i - 1))
                        dve.tensor_scalar(res[:, h1, :], y[:, h1, :], mv[:, h1, 0:1], rstd[:, h1, :],
                                          ALU.subtract, ALU.mult).then_inc(res_made, 1)
                    if this:
                        dve.wait_ge(eps_set, 1)
                        dve.wait_ge(stats_made, t + 1)
                        dve.bn_aggr(mv[:, h, :], stats[:, h, :]).then_inc(mv_made, 1)

                dve.memset(eps_sb[:, :], EPS).then_inc(eps_set, 1)
                at_tile(-2, 0, turn=False, this=False, last=False)
                at_tile(-1, 1, this=False, last=False)
                at_tile(0, 0, 0, last=False)
                at_tile(1, 1, 0)
                at_tile(2, 0, 1)
                at_tile(3, 1, 1)
                with dve.Fori(2, TILES // 2 - 1) as i:
                    for h in range(2):
                        at_tile(2 * i + h, h, i)
                at_tile(TILES - 2, 0, TILES // 2 - 1, start=False)
                at_tile(TILES - 1, 1, TILES // 2 - 1, start=False, turn=False)
                at_tile(TILES, 0, TILES // 2, start=False, turn=False, this=False)

            @block.tensor
            def _(pe):
                def turn(t, h):
                    pe.wait_ge(o_made, t + 1)
                    for kc in range(2):
                        last = pe.transpose(oT_ps[h][:, kc * P:(kc + 1) * P], o[:, h, kc * P:(kc + 1) * P], ident[:, :])
                    last.then_inc(oT_made, 1)

                def project(t, h, first=False):
                    pe.wait_ge(oT_staged, t + 1)
                    if not first:
                        pe.wait_ge(y_made, t - 1)
                    for kc in range(2):
                        pe.matmul(y_ps[h][:, 0:D], oT[:, h, kc * P:(kc + 1) * P], wo_sb[:, kc, :], start=kc == 0, stop=False)
                    pe.matmul(y_ps[h][:, 0:D], ones_b[:, :], bias_parts[:, PW:BW], start=False, stop=True).then_inc(proj_made, 1)

                turn(0, 0)
                turn(1, 1)
                for h in range(2):
                    project(h, h, first=True)
                    turn(2 + h, h)
                with pe.Fori(1, TILES // 2 - 1) as i:
                    for h in range(2):
                        project(2 * i + h, h)
                        turn(2 * i + 2 + h, h)
                for h in range(2):
                    project(TILES - 2 + h, h)

            @block.scalar
            def _(act):
                def deviation(t, h):
                    act.wait_ge(mv_made, t + 1)
                    act.activation(rstd[:, h, :], mv[:, h, 1:2], ACT.Sqrt, bias=eps_sb[:, :]).then_inc(std_made, 1)

                act.wait_ge(eps_set, 1)
                with act.Fori(0, TILES // 2) as i:
                    for h in range(2):
                        deviation(2 * i + h, h)

            @block.gpsimd
            def _(pool):
                for t in range(-2, TILES + 1):
                    if t + 2 < TILES:
                        if t >= 0:
                            pool.wait_ge(y_made, t + 1)
                        pool.indirect_dma_start(out=x[:, t % 2, :], out_offset=None, in_=x_rows,
                                                in_offset=bass.IndirectOffsetOnAxis(ap=node_id[:, t + 2:t + 3], axis=0),
                                                bounds_check=NP - 1, oob_is_err=False).then_inc(x_in[t % 2], 16)
                    if t >= 1:
                        pool.wait_ge(res_made, t)
                        pool.indirect_dma_start(out=out, out_offset=bass.IndirectOffsetOnAxis(ap=node_id[:, t - 1:t], axis=0),
                                                in_=res[:, (t - 1) % 2, :], in_offset=None,
                                                bounds_check=N - 1, oob_is_err=False).then_inc(out_done[(t - 1) % 2], 16)
                for h in range(2):
                    pool.wait_ge(out_done[h], 16 * TILES // 2)




def kernel(x, src, dst, L0_gnn_Wq, L0_gnn_bq, L0_gnn_Wk, L0_gnn_bk, L0_gnn_Wv, L0_gnn_bv, L0_gnn_Wo, L0_gnn_bo):
    import numpy as np
    import concourse.bacc as bacc
    from concourse.bass_utils import run_bass_kernel_spmd

    by_head = np.arange(D).reshape(HD, HEADS).T.reshape(-1)

    def contraction_first(w):
        return np.ascontiguousarray(np.asarray(w).reshape(2, P, -1).transpose(1, 0, 2))

    rows = np.zeros((NP, D), np.float32)
    rows[:N] = np.asarray(x)
    wq, wk, wv = (np.asarray(w)[by_head].T for w in (L0_gnn_Wq, L0_gnn_Wk, L0_gnn_Wv))
    arrays = {
        "x_rows": rows,
        "xT": contraction_first(rows.T),
        "src": np.ascontiguousarray(np.asarray(src).reshape(EP, EF)),
        "dst": np.ascontiguousarray(np.asarray(dst).reshape(EP, EF)),
        "wT": contraction_first(np.concatenate([wk, wv, wq], 1)),
        "bias": np.concatenate([np.asarray(b)[by_head] for b in (L0_gnn_bk, L0_gnn_bv, L0_gnn_bq)]
                               + [np.asarray(L0_gnn_bo)])[None],
        "woT": contraction_first(np.asarray(L0_gnn_Wo)[:, by_head].T),
    }
    nc = bacc.Bacc("TRN2", target_bir_lowering=False, num_devices=1)
    args = [nc.dram_tensor(f"in_{name}", a.shape, mybir.dt.from_np(a.dtype), kind="ExternalInput").ap() for name, a in arrays.items()]
    out = nc.dram_tensor("out_rows", (N, D), F32, kind="ExternalOutput").ap()
    gnn_kernel(nc, *args, out)
    r = run_bass_kernel_spmd(nc, [{f"in_{name}": a for name, a in arrays.items()}], core_ids=[0])
    return r.results[0]["out_rows"]
```

```python
from contextlib import ExitStack

import concourse.bass as bass
from concourse import mybir

P = 128
N, D, E = 12500, 256, 200000
HEADS = 8
HD = D // HEADS
TILES = (N + P - 1) // P
NP = TILES * P
QW = D + 1
VW = HEADS * (HD + 1)
KVW = D + VW
PW = 3 * D
BW = PW + D
R = 4
EP = 125
EF = E // EP
FBITS, PBITS = 11, 7
SF = 1 << FBITS
HALF, QUARTER = SF // 2, SF // 4
SLOTS = P * SF
ROW_SHIFT = 14
COL_MASK = (1 << ROW_SHIFT) - 1
KEY_BASE = 0x20000000
SENTINEL = KEY_BASE | (COL_MASK << ROW_SHIFT)
CH = 320
CHUNKS = EF // CH
POOL_HOTS = 28
CLIP = 1022
G = 3
QR = 2 * R
BP = 65
C = 39
TAB = TILES + 1
U = 6
V = G - 1
B = 6
STEPS = C // G + (E // P + (TILES - 1) * (G - 1)) // G
LOOPS = (STEPS - 2) // B
assert B % 2 == 0 and B % U == 0
NEG = -3.0e30
M0 = -1.0e30
SCALE = HD ** -0.5
EPS = 1e-5
RUNG = 14
assert TILES % RUNG == 0 and C % G == 0 and EF % CH == 0

F32, I32, BF16 = mybir.dt.float32, mybir.dt.int32, mybir.dt.bfloat16
ALU = mybir.AluOpType
ACT = mybir.ActivationFunctionType
AX = mybir.AxisListType


def prepare(nc, sem, x_rows, xT, src, dst, wT, bias, woT, kv_rows, node_rows, edge_keys, q_perm,
            ident, ones, upper, bias_parts, ones_b, wo_sb, node_id, start_f, tile_deg, gmax_i):
    with ExitStack() as ps:
        def sb(name, shape, dtype=F32):
            return ps.enter_context(nc.sbuf_tensor(name, shape, dtype))

        def pp(name, shape, dtype=F32):
            return ps.enter_context(nc.psum_tensor(name, shape, dtype))

        A = [sb("sort_a", [P, SF]), sb("sort_b", [P, SF])]
        src_sb = sb("src_sb", [EP, EF], I32)
        dst_sb = A[1][0:EP, 0:EF].bitcast(I32)
        hi_b, lo_b = sb("hi_b", [EP, EF], BF16), sb("lo_b", [EP, EF], BF16)
        hot_hi, hot_lo = sb("hot_hi", [EP, TILES, CH], BF16), sb("hot_lo", [EP, P, CH], BF16)
        digit = hot_hi[:, 0:2 * EF // CH, :].rearrange("p v e -> p (v e)").bitcast(I32)
        early_f = hot_lo[0:BP, :, :].rearrange("p v e -> p (v e)")
        bias_f, part = early_f[:, 0:2 * BW].bitcast(F32), early_f[:, 2 * BW:3 * BW]
        w_sb = sb("w_sb", [P, 2, PW])
        xt_sb = sb("xt_sb", [P, R, 2, P])
        kv_st, q_st = sb("kv_st", [P, R, KVW]), sb("q_st", [P, R, D])
        qg = kv_st[:, :, :].rearrange("p r w -> p (r w)").rearrange("p (r w) -> p r w", r=QR)
        pid, gray, sgn_i = sb("pid", [P, 1], I32), sb("gray", [P, 1], I32), sb("sgn_i", [P, 9], I32)
        sgn = sb("sgn", [P, 9])
        O = [sb("ord_a", [P, P]), sb("ord_b", [P, P])]
        nid_f, deg, excl = sb("nid_f", [P, P]), sb("deg", [P, P]), sb("excl", [P, P])
        start_i, ord_i = sb("start_i", [P, P], I32), sb("ord_i", [P, P], I32)
        row_sum, row_max, row_off, gmax_f = (sb(x, [P, 1]) for x in ("row_sum", "row_max", "row_off", "gmax_f"))

        hist_ps, misc_ps = pp("hist_ps", [P, 512]), pp("misc_ps", [P, 512])
        kv_ps = [pp("kv_ps0", [P, 512]), pp("kv_ps1", [P, 512])]
        q_ps = [pp("q_ps0", [P, 512]), pp("q_ps1", [P, 512])]
        T_ps = [pp("T_ps0", [P, QUARTER]), pp("T_ps1", [P, QUARTER])]

        src_in, dst_in, w_in, bias_in, wo_in, consts, digits = (
            sem(x) for x in ("src_in", "dst_in", "w_in", "bias_in", "wo_in", "consts", "digits"))
        hots_made, pool_hots_made, hot_used = sem("hots_made"), sem("pool_hots_made"), sem("hot_used")
        sort_done = sem("sort_done")
        offs_made, ord_turned, nodes_ready = sem("offs_made"), sem("ord_turned"), sem("nodes_ready")
        starts_ready, starts_out = sem("starts_ready"), sem("starts_out")
        xt_in, kv_out, q_out = ([sem(f"{x}{j}") for j in range(R)] for x in ("xt_in", "kv_out", "q_out"))
        kv_made, kv_staged = sem("kv_made"), sem("kv_staged")
        turned, unturned = sem("turned"), sem("unturned")
        qg_in, qg_out = ([sem(f"{x}{j}") for j in range(QR)] for x in ("qg_in", "qg_out"))
        start_taken = sem("start_taken")
        keys_out, idle_out = sem("keys_out"), sem("idle_out")

        SPAN = range(FBITS + 1, FBITS + PBITS + 1)
        HOT_AT = {1: 0, 5: 1, 7: 2, 8: 3, 9: 4}
        ORDER_AT = 10
        BODIES = TILES // R
        EARLY, MIDDLE = [3, 3, 2, 2, 0], 4
        AFTER_TURN = {1: 1, 3: 1, 5: 1, 9: 1}
        AFTER_PHASE = {13: 1, 14: 1, 15: 2, 16: 2}
        assert sum(EARLY) + MIDDLE + sum(AFTER_TURN.values()) + sum(AFTER_PHASE.values()) == BODIES
        at = {}
        order_T = []
        halves = []

        with nc.Block() as block:

            @block.vector
            def _(dve):
                n = [0]
                mine = {"edges": 0, "nodes": 0}

                def did(ins, who="edges"):
                    n[0] += 1
                    mine[who] = n[0]
                    ins.then_inc(sort_done, 1)

                def settle(who="edges"):
                    dve.wait_ge(sort_done, mine[who])

                def stage(bufs, c, lo, width, bit):
                    a, b = (bufs[x][:, lo:lo + width].rearrange("p (m two j) -> p m two j", two=2, j=1 << bit) for x in (c, 1 - c))
                    settle()
                    did(dve.tensor_tensor(b[:, :, 0, :], a[:, :, 0, :], a[:, :, 1, :], ALU.min))
                    beside()
                    did(dve.tensor_tensor(b[:, :, 1, :], a[:, :, 0, :], a[:, :, 1, :], ALU.max))
                    beside()
                    return 1 - c

                def flip(t, by=-1.0):
                    settle()
                    did(dve.tensor_scalar(t, t, by, None, ALU.mult))

                def flip_after(t, width, k):
                    w = (width - 1).bit_length()
                    if k < w - 1:
                        flip(t[:, 0:width].rearrange("p (m w) -> p m w", w=4 << k)[:, :, 1 << k:3 << k])
                    elif k == w - 1:
                        flip(t[:, 0:width // 2], sgn[:, 7:8])
                        flip(t[:, width // 2:width], sgn[:, 8:9])

                def hot_chunk(c):
                    if c:
                        dve.wait_ge(hot_used, c)
                    for v in range(P):
                        dve.tensor_scalar(hot_lo[:, v, :], lo_b[:, c * CH:(c + 1) * CH], float(v), None, ALU.is_equal)
                    for v in range(POOL_HOTS, TILES):
                        last = dve.tensor_scalar(hot_hi[:, v, :], hi_b[:, c * CH:(c + 1) * CH], float(v), None, ALU.is_equal)
                    last.then_inc(hots_made, 1)

                keys = A[0][0:EP, 0:EF].bitcast(I32)
                did(dve.memset(A[0][:, :].bitcast(I32), SENTINEL))
                did(dve.memset(bias_f[:, :], 0.0))
                did(dve.memset(ones_b[:, :], 1.0))
                at["cleared"] = n[0]
                for h in range(R):
                    did(dve.memset(kv_st[:, h, D:KVW].rearrange("p (g w) -> p g w", w=HD + 1)[:, :, HD:HD + 1], 1.0))
                at["ones"] = n[0]
                dve.wait_ge(src_in, 16)
                did(dve.tensor_scalar(digit, src_sb[:, :], PBITS, None, ALU.logical_shift_right))
                settle()
                dve.tensor_copy(hi_b[:, :], digit).then_inc(digits, 1)
                dve.wait_ge(digits, 1)
                did(dve.tensor_scalar(digit, src_sb[:, :], P - 1, None, ALU.bitwise_and))
                settle()
                dve.tensor_copy(lo_b[:, :], digit).then_inc(digits, 1)
                did(dve.tensor_scalar(keys, src_sb[:, :], ROW_SHIFT, KEY_BASE, ALU.logical_shift_left, ALU.bitwise_or))
                dve.wait_ge(dst_in, 16)
                settle()
                did(dve.tensor_tensor(keys, keys, dst_sb, ALU.bitwise_or))
                dve.wait_ge(bias_in, 48)
                did(dve.tensor_copy(bias_parts[:, :], bias_f[:, :]))
                settle()
                did(dve.tensor_tensor(bias_f[:, :], bias_f[:, :], bias_parts[:, :], ALU.subtract))
                settle()
                did(dve.tensor_copy(part[:, :], bias_f[:, :]))
                settle()
                did(dve.tensor_tensor(bias_f[:, :], bias_f[:, :], part[:, :], ALU.subtract))
                did(dve.tensor_copy(bias_parts[32:33, :], part[32:33, :]))
                settle()
                did(dve.tensor_copy(bias_parts[64:65, :], bias_f[64:65, :]))
                at["bias"] = n[0]
                dve.wait_ge(consts, 7)
                did(dve.tensor_scalar(gray[:, :], pid[:, :], 1, None, ALU.logical_shift_right))
                settle()
                did(dve.tensor_tensor(gray[:, :], gray[:, :], pid[:, :], ALU.bitwise_xor))
                settle()
                for a in range(PBITS):
                    did(dve.tensor_scalar(sgn_i[:, a:a + 1], gray[:, :], a, 1, ALU.logical_shift_right, ALU.bitwise_and))
                did(dve.tensor_scalar(sgn_i[:, 7:8], pid[:, :], 1, None, ALU.bitwise_and))
                settle()
                did(dve.tensor_scalar(sgn[:, 0:8], sgn_i[:, 0:8], -2.0, 1.0, ALU.mult, ALU.add))
                settle()
                did(dve.tensor_scalar(sgn[:, 8:9], sgn[:, 7:8], -1.0, None, ALU.mult))
                dve.wait_ge(digits, 2)

                def order_nodes():
                    def did_(ins):
                        did(ins, "nodes")

                    def settle_():
                        settle("nodes")

                    dve.wait_ge(hot_used, CHUNKS)
                    did_(dve.memset(deg[:, :], 0.0))
                    yield
                    settle_()
                    did_(dve.tensor_copy(deg[0:TILES, :], hist_ps[0:TILES, 0:P]))
                    yield
                    settle_()
                    did_(dve.tensor_tensor_scan(excl[:, :], ones[:, :], deg[:, :], 0.0, ALU.mult, ALU.add))
                    did_(dve.tensor_reduce(row_max[:, :], deg[:, :], AX.X, ALU.max))
                    yield
                    settle_()
                    did_(dve.tensor_copy(row_sum[:, :], excl[:, P - 1:P]))
                    at["row_sum"] = n[0]
                    settle_()
                    did_(dve.tensor_tensor(excl[:, :], excl[:, :], deg[:, :], ALU.subtract))
                    did_(dve.tensor_scalar(deg[:, :], deg[:, :], float(CLIP), -1.0, ALU.min, ALU.mult))
                    did_(dve.tensor_scalar(O[1][:, :], nid_f[:, :], float(N), float((CLIP + 1) << ROW_SHIFT), ALU.is_ge, ALU.mult))
                    yield
                    settle_()
                    did_(dve.tensor_scalar(deg[:, :], deg[:, :], float(CLIP), float(1 << ROW_SHIFT), ALU.add, ALU.mult))
                    yield
                    settle_()
                    did_(dve.tensor_tensor(deg[:, :], deg[:, :], O[1][:, :], ALU.max))
                    yield
                    settle_()
                    did_(dve.tensor_tensor(O[0][:, :], deg[:, :], nid_f[:, :], ALU.add))
                    yield
                    dve.wait_ge(offs_made, 1)
                    did_(dve.tensor_copy(row_off[:, :], misc_ps[:, 256:257]))
                    did_(dve.tensor_reduce(gmax_f[0:1, :], misc_ps[0:1, 128:256], AX.X, ALU.max))
                    yield
                    settle_()
                    did_(dve.tensor_copy(gmax_i[:, :], gmax_f[0:1, :]))
                    dve.tensor_scalar(start_i[:, :], excl[:, :], row_off[:, :], None, ALU.add).then_inc(starts_ready, 1)
                    early = O[0][:, :].rearrange("p (m w) -> p m w", w=4)[:, :, 2:4]
                    did_(dve.tensor_scalar(early, early, -1.0, None, ALU.mult))
                    o = 0
                    for k in range(1, 2 * PBITS + 1):
                        for bits, turns in ((range(k - PBITS - 1, -1, -1), True), (range(min(k, PBITS) - 1, -1, -1), False)):
                            if k > PBITS:
                                order_T.append((o, mine["nodes"]))
                                yield
                                yield
                                dve.wait_ge(ord_turned, len(order_T))
                                did_(dve.tensor_copy(O[1 - o][:, :], misc_ps[:, 0:P]))
                                o = 1 - o
                                yield
                            elif turns:
                                continue
                            for bit in bits:
                                a, b = (O[x][:, :].rearrange("p (m two j) -> p m two j", two=2, j=1 << bit) for x in (o, 1 - o))
                                settle_()
                                did_(dve.tensor_tensor(b[:, :, 0, :], a[:, :, 0, :], a[:, :, 1, :], ALU.min))
                                did_(dve.tensor_tensor(b[:, :, 1, :], a[:, :, 0, :], a[:, :, 1, :], ALU.max))
                                o = 1 - o
                                yield
                        settle_()
                        if k < PBITS - 1:
                            part_ = O[o][:, :].rearrange("p (m w) -> p m w", w=4 << k)[:, :, 1 << k:3 << k]
                            did_(dve.tensor_scalar(part_, part_, -1.0, None, ALU.mult))
                        elif k == PBITS - 1:
                            for h in range(2):
                                part_ = O[o][:, h * (P // 2):(h + 1) * (P // 2)]
                                did_(dve.tensor_scalar(part_, part_, sgn[:, 7 + h:8 + h], None, ALU.mult))
                        elif k < 2 * PBITS:
                            did_(dve.tensor_scalar(O[o][:, :], O[o][:, :], sgn[:, k - PBITS:k - PBITS + 1], None, ALU.mult))
                        yield
                    settle_()
                    did_(dve.tensor_copy(sgn_i[:, 8:9], O[o][:, 0:1]))
                    order_T.append((o, mine["nodes"]))
                    yield
                    yield
                    dve.wait_ge(ord_turned, len(order_T))
                    did_(dve.tensor_copy(ord_i[:, :], misc_ps[:, 0:P]))
                    yield
                    settle_()
                    dve.tensor_scalar(node_id[:, :], ord_i[:, :], COL_MASK, None, ALU.bitwise_and).then_inc(nodes_ready, 1)
                    did_(dve.tensor_scalar(sgn_i[:, 8:9], sgn_i[:, 8:9], ROW_SHIFT, None, ALU.logical_shift_right))
                    yield
                    settle_()
                    did_(dve.tensor_copy(tile_deg[:, :], sgn_i[:, 8:9]))
                    yield
                    settle_()
                    did_(dve.tensor_scalar(tile_deg[:, :], tile_deg[:, :], -1.0, float(CLIP), ALU.mult, ALU.add))
                    yield
                    settle_()
                    did_(dve.tensor_scalar(row_max[:, :], tile_deg[:, :], float(CLIP), float(E), ALU.is_ge, ALU.mult))
                    yield
                    settle_()
                    did_(dve.tensor_tensor(tile_deg[:, :], tile_deg[:, :], row_max[:, :], ALU.add))

                ordering = order_nodes()
                begun = [False]

                def beside():
                    if begun[0]:
                        next(ordering, None)

                flip(A[0][:, :].rearrange("p (m w) -> p m w", w=4)[:, :, 2:4])
                c = 0
                for k in range(1, FBITS + 1):
                    if k in HOT_AT:
                        hot_chunk(HOT_AT[k])
                    if k == ORDER_AT:
                        begun[0] = True
                    for bit in range(k - 1, -1, -1):
                        c = stage(A, c, 0, SF, bit)
                    if k < FBITS:
                        flip_after(A[c], SF, k)
                for h in range(2):
                    flip(A[c][:, h * HALF:(h + 1) * HALF], sgn[:, 0:1])
                at[FBITS + 1, "to", 0] = at[FBITS + 1, "to", 1] = n[0]

                for k in SPAN:
                    there = 1 - c
                    for h in range(2):
                        o = there
                        dve.wait_ge(unturned, 8 * (k - SPAN[0]) + 2 * h + 2)
                        for bit in range(k - FBITS - 1, -1, -1):
                            o = stage(A, o, h * HALF, HALF, bit)
                        at[k, "back", h] = n[0]
                    halves.append(((c, there), (o, 1 - o)))
                    c = 1 - o
                    dve.wait_ge(unturned, 8 * (k - SPAN[0]) + 8)
                    c = stage(A, c, 0, SF, FBITS - 1)
                    for h in range(2):
                        o = c
                        for bit in range(FBITS - 2, -1, -1):
                            o = stage(A, o, h * HALF, HALF, bit)
                        if k != SPAN[-1]:
                            flip(A[o][:, h * HALF:(h + 1) * HALF], sgn[:, k - FBITS:k - FBITS + 1])
                            at[k + 1, "to", h] = n[0]
                    c = o
                for _ in ordering:
                    pass
                at["keys"] = (n[0], c)

            work = []
            turns = [(value, "nodes", i) for i, (o, value) in enumerate(order_T)]
            quarters = [(at[k, way, r // 2], "quarter", (k, way, r)) for k in SPAN for way in ("to", "back") for r in range(4)]
            done = sum(EARLY) + MIDDLE
            for value, what, which in sorted(turns + quarters, key=lambda ask: ask[0]):
                work.append((what, which))
                more = AFTER_TURN.get(which, 0) if what == "nodes" else AFTER_PHASE.get(which[0], 0) if which[1:] == ("back", 3) else 0
                if more:
                    work.append(("bodies", (done, done + more)))
                    done += more
                    if done == BODIES:
                        work.append(("tiles", range(BODIES * R, TILES)))

            @block.sync
            def _(sp):
                sp.dma_start(src_sb[:, :], src).then_inc(src_in, 16)
                sp.dma_start(dst_sb, dst).then_inc(dst_in, 16)
                sp.dma_start(w_sb[:, :, :], wT).then_inc(w_in, 16)
                sp.wait_ge(sort_done, at["cleared"])
                for p in (0, 32, 64):
                    sp.dma_start(bias_f[p:p + 1, :], bias).then_inc(bias_in, 16)
                sp.dma_start(wo_sb[:, :, :], woT).then_inc(wo_in, 16)
                sp.dma_start(q_perm[NP:NP + P, :], x_rows[0:P, :]).then_inc(idle_out, 16)

                def load_x(t, j):
                    sp.dma_start(xt_sb[:, j, :, :], xT[:, :, bass.ds(t * P, P)]).then_inc(xt_in[j], 16)

                def store_rows(t, j):
                    sp.wait_ge(kv_staged, t + 1)
                    sp.dma_start(kv_rows[bass.ds(t * P, P), :], kv_st[:, j, :]).then_inc(kv_out[j], 16)
                    sp.dma_start(node_rows[bass.ds(t * P, P), 0:D], q_st[:, j, :]).then_inc(q_out[j], 16)

                for j in range(R):
                    load_x(j, j)
                with sp.Fori(0, BODIES - 1) as i:
                    for j in range(R):
                        sp.wait_ge(kv_made, i * R + j + 1)
                        load_x(i * R + j + R, j)
                        store_rows(i * R + j, j)
                for t in range(BODIES * R - R, TILES):
                    if t + R < TILES:
                        sp.wait_ge(kv_made, t + 1)
                        load_x(t + R, t % R)
                    store_rows(t, t % R)
                sp.wait_ge(starts_ready, 1)
                sp.dma_start(node_rows[:, D:D + 1].rearrange("(p f) one -> p (f one)", f=P),
                             start_i[0:TILES, :].bitcast(F32), allow_slow_non_contiguous=True).then_inc(starts_out, 16)

                def store_q(t, j, turn):
                    sp.wait_ge(qg_in[j], 16 * turn + 16)
                    sp.dma_start(q_perm[bass.ds(t * P, P), :], qg[:, j, 0:D]).then_inc(qg_out[j], 16)

                with sp.Fori(0, TILES // QR) as i:
                    for j in range(QR):
                        store_q(i * QR + j, j, i)
                for t in range(TILES // QR * QR, TILES):
                    store_q(t, t % QR, TILES // QR)
                sp.wait_ge(sort_done, at["keys"][0])
                sp.dma_start(edge_keys.rearrange("(p f) one -> p (f one)", f=SF), A[at["keys"][1]][:, :].bitcast(I32)).then_inc(keys_out, 16)
                sp.wait_ge(wo_in, 16)
                sp.wait_ge(idle_out, 16)
                sp.wait_ge(keys_out, 16)
                for j in range(R):
                    sp.wait_ge(kv_out[j], 16 * len(range(j, TILES, R)))
                    sp.wait_ge(q_out[j], 16 * len(range(j, TILES, R)))
                for j in range(QR):
                    sp.wait_ge(qg_out[j], 16 * len(range(j, TILES, QR)))

            @block.gpsimd
            def _(pool):
                pool.memset(ident[:, :], 0.0).then_inc(consts, 1)
                pool.memset(upper[:, :], 1.0).then_inc(consts, 1)
                pool.memset(ones[:, :], 1.0).then_inc(consts, 1)
                pool.wait_ge(consts, 3)
                pool.affine_select(out=ident[:, :], in_=ident[:, :], compare_op=ALU.not_equal, fill=1.0, base=0,
                                   pattern=[[-1, P]], channel_multiplier=1).then_inc(consts, 1)
                pool.affine_select(out=upper[:, :], in_=upper[:, :], compare_op=ALU.is_gt, fill=0.0, base=0,
                                   pattern=[[1, P]], channel_multiplier=-1).then_inc(consts, 1)
                pool.iota(pid[:, :], pattern=[[0, 1]], base=0, channel_multiplier=1).then_inc(consts, 1)
                pool.iota(nid_f[:, :], pattern=[[1, P]], base=0, channel_multiplier=P,
                          allow_small_or_imprecise_dtypes=True).then_inc(consts, 1)
                pool.wait_ge(digits, 2)
                for c in range(CHUNKS):
                    if c:
                        pool.wait_ge(hot_used, c)
                    for v in range(POOL_HOTS):
                        last = pool.tensor_scalar(hot_hi[:, v, :], hi_b[:, c * CH:(c + 1) * CH], float(v), None, ALU.is_equal)
                    last.then_inc(pool_hots_made, 1)
                pool.wait_ge(nodes_ready, 1)
                for j in range(R):
                    pool.wait_ge(q_out[j], 16 * len(range(j, TILES, R)))
                    pool.wait_ge(kv_out[j], 16 * len(range(j, TILES, R)))
                pool.wait_ge(starts_out, 16)

                def take_starts(u):
                    most = min(R, TILES - u)
                    for t in range(u, u + most):
                        pool.wait_ge(qg_in[t % QR], 16 * (t // QR) + 16)
                    pool.tensor_copy(start_f[:, u:u + most].unsqueeze(2), qg[:, u % QR:u % QR + most, D:QW].bitcast(I32)).then_inc(start_taken, 1)

                for t in range(TILES):
                    if t >= QR:
                        pool.wait_ge(qg_out[t % QR], 16 * (t // QR))
                        pool.wait_ge(start_taken, (t - QR) // R + 1)
                    pool.indirect_dma_start(out=qg[:, t % QR, 0:QW], out_offset=None, in_=node_rows,
                                            in_offset=bass.IndirectOffsetOnAxis(ap=node_id[:, t:t + 1], axis=0),
                                            bounds_check=NP - 1, oob_is_err=False).then_inc(qg_in[t % QR], 16)
                    if t >= QR - 1 and t % R == R - 1:
                        take_starts(t - QR + 1)
                for u in range(TILES // R * R - R, TILES, R):
                    take_starts(u)

            @block.tensor
            def _(pe):
                def count_chunk(c):
                    pe.wait_ge(hots_made, c + 1)
                    pe.wait_ge(pool_hots_made, c + 1)
                    for e in range(CH):
                        last = pe.matmul(hist_ps[0:TILES, 0:P], hot_hi[:, :, e], hot_lo[:, :, e],
                                         start=c == 0 and e == 0, stop=c == CHUNKS - 1 and e == CH - 1)
                    last.then_inc(hot_used, 1)

                def project(t, j, turn, first=False):
                    pe.wait_ge(xt_in[j], 16 * turn + 16)
                    if not first:
                        pe.wait_ge(kv_staged, t - 1)
                    for ps, a, b in ((kv_ps[j % 2], 0, 2 * D), (q_ps[j % 2], 2 * D, PW)):
                        for kc in range(2):
                            pe.matmul(ps[:, 0:b - a], xt_sb[:, j, kc, :], w_sb[:, kc, a:b], start=kc == 0, stop=False)
                        last = pe.matmul(ps[:, 0:b - a], ones_b[:, :], bias_parts[:, a:b], start=False, stop=True)
                    last.then_inc(kv_made, 1)

                def project_bodies(a, b):
                    if a == 0:
                        for j in range(R):
                            project(j, j, 0, first=j < 2)
                    if b > max(a, 1):
                        with pe.Fori(max(a, 1), b) as i:
                            for j in range(R):
                                project(i * R + j, j, i)

                pe.wait_ge(consts, 7)
                done = 0
                for c in range(CHUNKS):
                    count_chunk(c)
                    if c == 0:
                        pe.wait_ge(w_in, 16)
                        pe.wait_ge(sort_done, at["bias"])
                    project_bodies(done, done + EARLY[c])
                    done += EARLY[c]
                pe.wait_ge(sort_done, at["row_sum"])
                pe.matmul(misc_ps[:, 256:257], upper[:, :], row_sum[:, :], start=True, stop=True)
                pe.matmul(misc_ps[0:1, 128:256], row_max[:, :], ident[:, :], start=True, stop=True).then_inc(offs_made, 1)
                project_bodies(done, done + MIDDLE)
                def turn_quarter(k, way, r):
                    count = 8 * (k - SPAN[0]) + 4 * (way == "back") + r
                    pe.wait_ge(sort_done, at[k, way, r // 2])
                    if count >= 2:
                        pe.wait_ge(unturned, count - 1)
                    a = A[halves[k - SPAN[0]][way == "back"][0]]
                    for b in range(QUARTER // P):
                        last = pe.transpose(T_ps[r % 2][:, b * P:(b + 1) * P],
                                            a[:, r * QUARTER + b * P:r * QUARTER + (b + 1) * P], ident[:, :])
                    last.then_inc(turned, 1)

                for what, which in work:
                    if what == "nodes":
                        pe.wait_ge(sort_done, order_T[which][1])
                        pe.transpose(misc_ps[:, 0:P], O[order_T[which][0]][:, :], ident[:, :]).then_inc(ord_turned, 1)
                    elif what == "quarter":
                        turn_quarter(*which)
                    elif what == "bodies":
                        project_bodies(*which)
                    else:
                        for t in which:
                            project(t, t % R, BODIES)

            @block.scalar
            def _(act):
                def stage_rows(t, j, turn, first=False):
                    act.wait_ge(kv_made, t + 1)
                    if not first:
                        act.wait_ge(kv_out[j], 16 * turn)
                        act.wait_ge(q_out[j], 16 * turn)
                    act.activation(kv_st[:, j, 0:D], kv_ps[j % 2][:, 0:D], ACT.Copy)
                    act.activation(kv_st[:, j, D:KVW].rearrange("p (g w) -> p g w", w=HD + 1)[:, :, 0:HD],
                                   kv_ps[j % 2][:, D:2 * D].rearrange("p (g w) -> p g w", w=HD), ACT.Copy)
                    act.activation(q_st[:, j, :], q_ps[j % 2][:, 0:D], ACT.Copy, scale=SCALE).then_inc(kv_staged, 1)

                def stage_bodies(a, b):
                    if a == 0:
                        for j in range(R):
                            stage_rows(j, j, 0, first=True)
                    if b > max(a, 1):
                        with act.Fori(max(a, 1), b) as i:
                            for j in range(R):
                                stage_rows(i * R + j, j, i)

                act.wait_ge(sort_done, at["ones"])
                stage_bodies(0, sum(EARLY) + MIDDLE)

                def unturn_quarter(k, way, r):
                    act.wait_ge(turned, 8 * (k - SPAN[0]) + 4 * (way == "back") + r + 1)
                    b = A[halves[k - SPAN[0]][way == "back"][1]]
                    act.activation(b[:, r * QUARTER:(r + 1) * QUARTER], T_ps[r % 2][:, :], ACT.Copy).then_inc(unturned, 1)

                for what, which in work:
                    if what == "quarter":
                        unturn_quarter(*which)
                    elif what == "bodies":
                        stage_bodies(*which)
                    elif what == "tiles":
                        for t in which:
                            stage_rows(t, t % R, BODIES)


def bounded(eng, value, most):
    return eng.snap(value).with_bounds(min_val=0, max_val=most)


def gnn_kernel(nc, x_rows, xT, src, dst, wT, bias, woT, out):
    with ExitStack() as ctx:
        def sb(name, shape, dtype=F32):
            return ctx.enter_context(nc.sbuf_tensor(name, shape, dtype))

        def sem(name):
            return ctx.enter_context(nc.semaphore(name))

        kv_rows = nc.dram_tensor("kv_rows", (NP, KVW), F32).ap()
        node_rows = nc.dram_tensor("node_rows", (NP, QW), F32).ap()
        edge_keys = nc.dram_tensor("edge_keys", (SLOTS, 1), I32).ap()
        q_perm = nc.dram_tensor("q_perm", (TAB * P, D), F32).ap()

        ident, ones, upper = sb("ident", [P, P]), sb("ones", [P, P]), sb("upper", [P, P])
        wo_sb = sb("wo_sb", [P, 2, D])
        bias_parts, ones_b = sb("bias_parts", [BP, BW], BF16), sb("ones_b", [BP, P], BF16)
        node_id = sb("node_id", [P, P], I32)
        start_f = sb("start_f", [P, TILES])
        tile_deg = sb("tile_deg", [P, 1])
        gmax_i = sb("gmax_i", [1, 1], I32)

        prepare(nc, sem, x_rows, xT, src, dst, wT, bias, woT, kv_rows, node_rows, edge_keys, q_perm,
                ident, ones, upper, bias_parts, ones_b, wo_sb, node_id, start_f, tile_deg, gmax_i)

        acc = sb("acc", [P, TAB * VW])
        runmax = sb("runmax", [P, TAB * HEADS])
        cols, mask = sb("cols", [P, TAB, C], I32), sb("mask", [P, TAB, C])
        step_tab = sb("step_tab", [1, STEPS + 1], I32)
        round_base = sb("round_base", [P, 1])

        acc_zeroed = sem("acc_zeroed")
        CUTS = TAB * VW * 3 // 10, TAB * VW * 6 // 10
        with nc.Block() as block:
            @block.vector
            def _(dve):
                dve.memset(acc[:, 0:CUTS[0]], 0.0)
                dve.memset(runmax[:, :], M0)
                dve.memset(round_base[:, :], 0.0)
                dve.memset(mask[:, TILES, :], NEG)
                dve.memset(cols[:, TILES, :], 0).then_inc(acc_zeroed, 1)

            @block.gpsimd
            def _(pool):
                pool.memset(acc[:, CUTS[0]:CUTS[1]], 0.0).then_inc(acc_zeroed, 1)

            @block.scalar
            def _(act):
                act.activation(acc[:, CUTS[1]:], ones[:, 0:1].to_broadcast([P, TAB * VW - CUTS[1]]), ACT.Copy,
                               scale=0.0).then_inc(acc_zeroed, 1)

        gmax = nc.values_load(gmax_i[0:1, 0:1], min_val=1, max_val=E)
        with nc.Fori(0, (gmax + (C - 1)) // C):
            one_round(nc, sem, kv_rows, edge_keys, q_perm, ident, ones, upper, node_id, start_f, tile_deg,
                      acc, runmax, cols, mask, step_tab, round_base)
        finish(nc, sem, out, x_rows, ident, bias_parts, ones_b, wo_sb, node_id, acc)


def one_round(nc, new_sem, kv_rows, edge_keys, q_perm, ident, ones, upper, node_id, start_f, tile_deg,
              acc, runmax, cols, mask, step_tab, round_base):
    used = []

    def sem(name):
        used.append(new_sem(name))
        return used[-1]

    with ExitStack() as ps:
        def sb(name, shape, dtype=F32):
            return ps.enter_context(nc.sbuf_tensor(name, shape, dtype))

        def pp(name, shape, dtype=F32):
            return ps.enter_context(nc.psum_tensor(name, shape, dtype))

        run_at = sb("run_at", [P, TILES], I32)
        rows = sb("rows", [P, RUNG, C], I32)
        rem, nsteps, ends = sb("rem", [P, 1]), sb("nsteps", [P, 1]), sb("ends", [P, 1])
        thresh = sb("thresh", [P, C // G])
        tile_tab = sb("tile_tab", [1, STEPS], I32)
        idx = sb("idx", [P, U, G], I32)
        kv = sb("kv", [P, U, G, KVW])
        q = sb("q", [P, U, D])
        prod = sb("prod", [P, G, D])
        s = sb("s", [P, 2, (G + 1) * HEADS])
        pv = sb("pv", [P, 2, (G + 1) * VW])
        room = pv[:, :, :].rearrange("p b w -> p (b w)")
        step_f, past, tile_f = room[:, 0:STEPS], room[:, STEPS:2 * STEPS], room[0:1, 2 * STEPS:3 * STEPS]
        place_f = prod[0:1, :, :].rearrange("p g d -> p (g d)")[:, 0:STEPS]
        tab_ps = [pp("tab_ps0", [1, 512]), pp("tab_ps1", [1, 512]), pp("tab_ps2", [1, 512]), pp("tab_ps3", [1, 512])]
        end_ps = pp("end_ps", [P, 512])
        sum_ps = [pp("sum_ps0", [P, 512]), pp("sum_ps1", [P, 512])]

        plan = sem("plan")
        iotas, ends_made, counts_made, tab_ready = sem("iotas"), sem("ends_made"), sem("counts_made"), sem("tab_ready")
        runs_in = [sem(f"runs_in{i}") for i in range(TILES // RUNG)]
        run_at_ready, runs_ready = sem("run_at_ready"), sem("runs_ready")
        idx_ready, kv_in, q_in = sem("idx_ready"), [sem(f"kv_in{j}") for j in range(U)], [sem(f"q_in{j}") for j in range(U)]
        prod_made, scored, old_copied, masked, max_made, diffs_made = (
            sem(x) for x in ("prod_made", "scored", "old_copied", "masked", "max_made", "diffs_made"))
        exp_made, pv_made, last_made, carry_made, summed, acc_stored = (
            sem(x) for x in ("exp_made", "pv_made", "last_made", "carry_made", "summed", "acc_stored"))
        CUT = 512
        pieces = [(a, min(a + CUT, STEPS)) for a in range(0, STEPS, CUT)]
        at = {}

        with nc.Block() as block:

            @block.vector
            def _(dve):
                n = [0]

                def did(ins):
                    n[0] += 1
                    ins.then_inc(plan, 1)

                def settle():
                    dve.wait_ge(plan, n[0])

                did(dve.tensor_scalar(rem[:, :], round_base[:, :], -1.0, None, ALU.mult))
                dve.tensor_scalar(run_at[:, :], start_f[:, :], round_base[:, :], float(SLOTS - C), ALU.add, ALU.min).then_inc(run_at_ready, 1)
                settle()
                did(dve.tensor_scalar(rem[:, :], tile_deg[:, :], rem[:, :], float(C), ALU.add, ALU.min))
                dve.wait_ge(iotas, 2)
                settle()
                did(dve.tensor_scalar(thresh[:, :], thresh[:, :], rem[:, :], None, ALU.is_lt))
                settle()
                did(dve.tensor_reduce(nsteps[:, :], thresh[:, :], AX.X, ALU.add))
                at["nsteps"] = n[0] 
                dve.wait_ge(ends_made, 1)
                did(dve.tensor_copy(ends[:, :], end_ps[:, 0:1]))
                settle()
                did(dve.tensor_scalar(past, step_f, ends[:, :], None, ALU.is_ge))
                at["past"] = n[0]
                dve.wait_ge(counts_made, 1)
                for j, (a, b) in enumerate(pieces):
                    did(dve.tensor_copy(tile_f[:, a:b], tab_ps[2 * j][:, 0:b - a]))
                    did(dve.tensor_tensor(place_f[:, a:b], step_f[0:1, a:b], tab_ps[2 * j + 1][:, 0:b - a], ALU.subtract))
                settle()
                did(dve.tensor_copy(tile_tab[:, :], tile_f))
                did(dve.tensor_scalar(place_f, place_f, float(G), float(C - G), ALU.mult, ALU.min))
                settle()
                did(dve.scalar_tensor_tensor(place_f, tile_f, float(C), place_f, ALU.mult, ALU.add))
                settle()
                did(dve.scalar_tensor_tensor(place_f, place_f, float(P), tile_f, ALU.mult, ALU.add))
                settle()
                did(dve.memset(step_tab[:, STEPS:], TILES))
                settle()
                dve.tensor_copy(step_tab[:, 0:STEPS], place_f).then_inc(tab_ready, 1)

                for r in range(TILES // RUNG):
                    dve.wait_ge(runs_in[r], 16 * RUNG)
                    part = cols[:, r * RUNG:(r + 1) * RUNG, :]
                    mpart = mask[:, r * RUNG:(r + 1) * RUNG, :]
                    did(dve.tensor_scalar(rows[:, :, :], part, ROW_SHIFT, COL_MASK, ALU.logical_shift_right, ALU.bitwise_and))
                    did(dve.tensor_scalar(part, part, COL_MASK, None, ALU.bitwise_and))
                    settle()
                    did(dve.tensor_tensor(mpart, rows[:, :, :],
                                          node_id[:, r * RUNG:(r + 1) * RUNG].unsqueeze(2).to_broadcast([P, RUNG, C]), ALU.not_equal))
                    settle()
                    did(dve.tensor_scalar(mpart, mpart, NEG, None, ALU.mult))
                settle()
                dve.tensor_scalar(round_base[:, :], round_base[:, :], float(C), None, ALU.add).then_inc(runs_ready, 1)

                mflat = mask[:, :, :].rearrange("p t c -> p (t c)")

                def score(k, j, turn):
                    dve.wait_ge(kv_in[j], 16 * G * turn + 16 * G)
                    dve.wait_ge(q_in[j], 16 * turn + 16)
                    dve.tensor_tensor(prod[:, :, :], kv[:, j, :, 0:D], q[:, j, :].unsqueeze(1).to_broadcast([P, G, D]),
                                      ALU.mult).then_inc(prod_made, 1)

                def score_sum(k, b, peeled=False):
                    dve.wait_ge(prod_made, k + 1)
                    if not peeled:
                        dve.wait_ge(last_made, k - 1)
                    dve.tensor_reduce(s[:, b, 0:G * HEADS], prod[:, :, :].rearrange("p g (h d) -> p (g h) d", d=HD),
                                      AX.X, ALU.add).then_inc(scored, 1)

                def mask_scores(k, b, col, tile):
                    dve.tensor_copy(s[:, b, G * HEADS:], runmax[:, bass.ds(tile * HEADS, HEADS)]).then_inc(old_copied, 1)
                    dve.wait_ge(scored, k + 1)
                    sv = s[:, b, 0:G * HEADS].rearrange("p (g h) -> p g h", h=HEADS)
                    dve.tensor_tensor(sv, sv, mflat[:, bass.ds(col, G)].unsqueeze(2).to_broadcast([P, G, HEADS]), ALU.add).then_inc(masked, 1)

                def maxima(k, b, tile):
                    m = runmax[:, bass.ds(tile * HEADS, HEADS)]
                    dve.wait_ge(tab_ready, 1)
                    dve.wait_ge(old_copied, k + 1)
                    dve.wait_ge(masked, k + 1)
                    dve.tensor_reduce(m, s[:, b, :].rearrange("p (g h) -> p h g", h=HEADS), AX.X, ALU.max).then_inc(max_made, 1)

                def differences(k, b, tile):
                    m = runmax[:, bass.ds(tile * HEADS, HEADS)]
                    dve.wait_ge(max_made, k + 1)
                    sa = s[:, b, :].rearrange("p (g h) -> p g h", h=HEADS)
                    dve.tensor_tensor(sa, sa, m.unsqueeze(1).to_broadcast([P, G + 1, HEADS]), ALU.subtract).then_inc(diffs_made, 1)

                def weigh(k, j, b, peeled=False):
                    dve.wait_ge(exp_made, k + 1)
                    if not peeled:
                        dve.wait_ge(summed, k - 1)
                    dve.tensor_tensor(pv[:, b, 0:V * VW].rearrange("p (g h w) -> p g h w", g=V, w=HD + 1),
                                      kv[:, j, 0:V, D:KVW].rearrange("p g (h w) -> p g h w", w=HD + 1),
                                      s[:, b, 0:V * HEADS].rearrange("p (g h) -> p g h", h=HEADS).unsqueeze(3).to_broadcast([P, V, HEADS, HD + 1]),
                                      ALU.mult).then_inc(pv_made, 1)

                def carry(k, b, tile, first=False):
                    if not first:
                        dve.wait_ge(acc_stored, k)
                    dve.tensor_tensor(pv[:, b, G * VW:].rearrange("p (h w) -> p h w", w=HD + 1),
                                      acc[:, bass.ds(tile * VW, VW)].rearrange("p (h w) -> p h w", w=HD + 1),
                                      s[:, b, G * HEADS:].unsqueeze(2).to_broadcast([P, HEADS, HD + 1]), ALU.mult).then_inc(carry_made, 1)

                dve.wait_ge(tab_ready, 1)
                dve.wait_ge(runs_ready, 1)
                tile_r = [dve.alloc_register(f"tile_{b}") for b in range(2)]
                col_r = [dve.alloc_register(f"col_{b}") for b in range(2)]

                def look_up(k, b):
                    v = dve.value_load(step_tab[0:1, bass.ds(k, 1)], min_val=0, max_val=TAB * C * P - 1)
                    dve.reg_mov(tile_r[b], v & (P - 1))
                    dve.reg_mov(col_r[b], v >> PBITS)

                def step(k, j, turn, peel=False, last=False):
                    b, b1 = j % 2, (j + 1) % 2
                    score_sum(k + 1, b1, peeled=peel and j == 0)
                    weigh(k, j % U, b, peeled=peel and j < 2)
                    tile, tile1, col1 = bounded(dve, tile_r[b], TILES), bounded(dve, tile_r[b1], TILES), bounded(dve, col_r[b1], TAB * C - G)
                    look_up(k + 2, b)
                    mask_scores(k + 1, b1, col1, tile1)
                    carry(k, b, tile, first=peel and j == 0)
                    maxima(k + 1, b1, tile1)
                    if not last:
                        score(k + 2, (j + 2) % U, turn + (j + 2) // U)
                    differences(k + 1, b1, tile1)

                look_up(0, 0)
                look_up(1, 1)
                score(0, 0, 0)
                score_sum(0, 0, peeled=True)
                tile, col = bounded(dve, tile_r[0], TILES), bounded(dve, col_r[0], TAB * C - G)
                mask_scores(0, 0, col, tile)
                maxima(0, 0, tile)
                score(1, 1, 0)
                differences(0, 0, tile)
                for j in range(B):
                    step(j, j, 0, peel=True)
                with dve.Fori(1, LOOPS) as kk:
                    for j in range(B):
                        step(kk * B + j, j, kk * (B // U))
                for k in range(LOOPS * B, STEPS - 1):
                    step(k, k - LOOPS * B, LOOPS * (B // U), last=k == STEPS - 2)
                k = STEPS - 1
                weigh(k, k % U, k % 2)
                carry(k, k % 2, bounded(dve, tile_r[k % 2], TILES))
                for r in tile_r + col_r:
                    dve.free_register(r)

            @block.gpsimd
            def _(pool):
                pool.iota(thresh[:, :], pattern=[[G, C // G]], base=0, channel_multiplier=0,
                          allow_small_or_imprecise_dtypes=True).then_inc(iotas, 1)
                pool.iota(step_f, pattern=[[1, STEPS]], base=0, channel_multiplier=0,
                          allow_small_or_imprecise_dtypes=True).then_inc(iotas, 1)
                pool.wait_ge(run_at_ready, 1)
                for i in range(TILES):
                    pool.indirect_dma_start(out=cols[:, i, :], out_offset=None, in_=edge_keys,
                                            in_offset=bass.IndirectOffsetOnAxis(ap=run_at[:, i:i + 1], axis=0),
                                            bounds_check=SLOTS - 1, oob_is_err=False).then_inc(runs_in[i // RUNG], 16)


                freed = pool.alloc_register("freed")
                pool.reg_mov(freed, 1)

                def ready(k, first=False):
                    pool.wait_ge(idx_ready, k + 1)
                    if not first:
                        pool.wait_ge(pv_made, freed)
                        pool.wait_ge(last_made, freed)
                        pool.reg_add(freed, freed, 1)

                def gather(k, j, first=False, last=False):
                    for g in range(G):
                        if g == G - 1 and not last:
                            ready(k + 1, first=first)
                        pool.indirect_dma_start(out=kv[:, j, g, :], out_offset=None, in_=kv_rows,
                                                in_offset=bass.IndirectOffsetOnAxis(ap=idx[:, j, g:g + 1], axis=0),
                                                bounds_check=NP - 1, oob_is_err=False).then_inc(kv_in[j], 16)

                ready(0, first=True)
                for j in range(B):
                    gather(j, j % U, first=j + 1 < U)
                with pool.Fori(1, LOOPS) as kk:
                    for j in range(B):
                        gather(kk * B + j, j % U)
                for k in range(LOOPS * B, STEPS):
                    gather(k, k % U, last=k == STEPS - 1)
                pool.free_register(freed)

            @block.sync
            def _(sp):
                def load_q(k, j, first=False):
                    tile = sp.value_load(tile_tab[0:1, bass.ds(k, 1)], min_val=0, max_val=TILES)
                    if not first:
                        sp.wait_ge(prod_made, k - U + 1)
                    sp.dma_start(q[:, j, :], q_perm[bass.ds(tile * P, P), :]).then_inc(q_in[j], 16)

                sp.wait_ge(tab_ready, 1)
                for j in range(B):
                    load_q(j, j % U, first=j < U)
                with sp.Fori(1, LOOPS) as kk:
                    for j in range(B):
                        load_q(kk * B + j, j % U)
                for k in range(LOOPS * B, STEPS):
                    load_q(k, k % U)

            @block.scalar
            def _(act):
                cflat = cols[:, :, :].rearrange("p t c -> p (t c)")

                def indices(k, j, turn):
                    v = act.value_load(step_tab[0:1, bass.ds(k, 1)], min_val=0, max_val=TAB * C * P - 1)
                    col = bounded(act, v >> PBITS, TAB * C - G)
                    if not isinstance(turn, int) or turn:
                        act.wait_ge(kv_in[j], 16 * G * turn)
                    act.activation(idx[:, j, :], cflat[:, bass.ds(col, G)], ACT.Copy).then_inc(idx_ready, 1)

                def weights(k, b):
                    act.wait_ge(diffs_made, k + 1)
                    act.activation(s[:, b, :], s[:, b, :], ACT.Exp).then_inc(exp_made, 1)

                def weigh_last(k, j, turn, b, peeled=False):
                    act.wait_ge(exp_made, k + 1)
                    act.wait_ge(kv_in[j], 16 * G * turn + 16 * G)
                    if not peeled:
                        act.wait_ge(summed, k - 1)
                    for h in range(HEADS):
                        at_h = h * (HD + 1)
                        last = act.activation(pv[:, b, V * VW + at_h:V * VW + at_h + HD + 1], kv[:, j, V, D + at_h:D + at_h + HD + 1],
                                              ACT.Copy, scale=s[:, b, V * HEADS + h:V * HEADS + h + 1])
                    last.then_inc(last_made, 1)

                def store(k, b):
                    v = act.value_load(step_tab[0:1, bass.ds(k, 1)], min_val=0, max_val=TAB * C * P - 1)
                    tile = bounded(act, v & (P - 1), TILES)
                    act.wait_ge(summed, k + 1)
                    act.activation(acc[:, bass.ds(tile * VW, VW)], sum_ps[b][:, 0:VW], ACT.Copy).then_inc(acc_stored, 1)

                act.wait_ge(tab_ready, 1)
                act.wait_ge(runs_ready, 1)
                for j in range(U):
                    indices(j, j, 0)
                weights(0, 0)
                weigh_last(0, 0, 0, 0, peeled=True)
                for k in range(B):
                    indices(k + U, k % U, 1)
                    weights(k + 1, (k + 1) % 2)
                    store(k, k % 2)
                    weigh_last(k + 1, (k + 1) % U, (k + 1) // U, (k + 1) % 2, peeled=k == 0)
                with act.Fori(1, LOOPS - 1) as kk:
                    for j in range(B):
                        k = kk * B + j
                        indices(k + U, j % U, kk * (B // U) + j // U + 1)
                        weights(k + 1, (j + 1) % 2)
                        store(k, j % 2)
                        weigh_last(k + 1, (j + 1) % U, kk * (B // U) + (j + 1) // U, (j + 1) % 2)
                for k in range((LOOPS - 1) * B, STEPS - 1):
                    if k + U < STEPS:
                        indices(k + U, k % U, (k + U) // U)
                    weights(k + 1, (k + 1) % 2)
                    store(k, k % 2)
                    weigh_last(k + 1, (k + 1) % U, (k + 1) // U, (k + 1) % 2)
                store(STEPS - 1, (STEPS - 1) % 2)

            @block.tensor
            def _(pe):
                pe.wait_ge(plan, at["nsteps"])
                pe.matmul(end_ps[:, 0:1], upper[:, :], nsteps[:, :], start=True, stop=False)
                pe.matmul(end_ps[:, 0:1], ident[:, :], nsteps[:, :], start=False, stop=True).then_inc(ends_made, 1)
                pe.wait_ge(plan, at["past"])
                for j, (a, b) in enumerate(pieces):
                    pe.matmul(tab_ps[2 * j][:, 0:b - a], ones[0:TILES, 0:1], past[0:TILES, a:b], start=True, stop=True)
                    last = pe.matmul(tab_ps[2 * j + 1][:, 0:b - a], nsteps[0:TILES, :], past[0:TILES, a:b], start=True, stop=True)
                last.then_inc(counts_made, 1)

                def total(k, b):
                    pe.wait_ge(pv_made, k + 1)
                    for g in range(V):
                        pe.matmul(sum_ps[b][:, 0:VW], ident[:, :], pv[:, b, g * VW:(g + 1) * VW], start=g == 0, stop=False)
                    pe.wait_ge(carry_made, k + 1)
                    pe.matmul(sum_ps[b][:, 0:VW], ident[:, :], pv[:, b, G * VW:], start=False, stop=False)
                    pe.wait_ge(last_made, k + 1)
                    pe.matmul(sum_ps[b][:, 0:VW], ident[:, :], pv[:, b, V * VW:G * VW], start=False, stop=True).then_inc(summed, 1)

                with pe.Fori(0, LOOPS) as kk:
                    for j in range(B):
                        total(kk * B + j, j % 2)
                for k in range(LOOPS * B, STEPS):
                    total(k, k % 2)

        with nc.Block() as block:

            @block.gpsimd
            def _(pool):
                numbers = range(used[0].num, used[-1].num + 1)
                assert len(numbers) == len(used)
                pool.dma_reset(numbers)
                pool.sem_clear(numbers)


def finish(nc, sem, out, x_rows, ident, bias_parts, ones_b, wo_sb, node_id, acc):
    with ExitStack() as ps:
        def sb(name, shape, dtype=F32):
            return ps.enter_context(nc.sbuf_tensor(name, shape, dtype))

        def pp(name, shape, dtype=F32):
            return ps.enter_context(nc.psum_tensor(name, shape, dtype))

        x = sb("x", [P, 2, D])
        z = sb("z", [P, 2, HEADS])
        o, oT = sb("o", [P, 2, D]), sb("oT", [P, 2, D])
        y = sb("y", [P, 2, D])
        stats, mv, rstd = sb("stats", [P, 2, 6]), sb("mv", [P, 2, 2]), sb("rstd", [P, 2, 1])
        res = sb("res", [P, 2, D])
        oT_ps = [pp("oT_ps0", [P, 512]), pp("oT_ps1", [P, 512])]
        y_ps = [pp("y_ps0", [P, 512]), pp("y_ps1", [P, 512])]
        x_in, out_done = [sem("x_in0"), sem("x_in1")], [sem("out_done0"), sem("out_done1")]
        zmax, zinv, o_made, oT_made, oT_staged, proj_made, y_made, stats_made, mv_made, std_made, rstd_made, res_made, eps_set = (
            sem(n) for n in ("zmax", "zinv", "o_made", "oT_made", "oT_staged", "proj_made", "y_made", "stats_made",
                             "mv_made", "std_made", "rstd_made", "res_made", "eps_set"))
        eps_sb = sb("eps_sb", [P, 1])

        with nc.Block() as block:
            @block.vector
            def _(dve):
                def at_tile(t, h, pair):
                    inside = not isinstance(t, int)
                    h1 = 1 - h

                    def of(tile):
                        return acc[:, bass.ds(tile * VW, VW)].rearrange("p (g w) -> p g w", w=HD + 1)

                    if inside or 0 <= t + 2 < TILES:
                        dve.wait_ge(zmax, t + 3)
                        dve.reciprocal(z[:, h, :], z[:, h, :]).then_inc(zinv, 1)
                    if inside or 0 <= t + 1 < TILES:
                        dve.wait_ge(oT_made, t + 2)
                        dve.tensor_copy(oT[:, h1, :], oT_ps[h1][:, 0:D]).then_inc(oT_staged, 1)
                    if inside or t >= 1:
                        dve.wait_ge(std_made, t)
                        dve.reciprocal(rstd[:, h1, :], rstd[:, h1, :]).then_inc(rstd_made, 1)
                    if inside or 0 <= t + 2 < TILES:
                        dve.wait_ge(zinv, t + 3)
                        dve.tensor_tensor(o[:, h, :].rearrange("p (g w) -> p g w", w=HD), of(t + 2)[:, :, 0:HD],
                                          z[:, h, :].unsqueeze(2).to_broadcast([P, HEADS, HD]), ALU.mult).then_inc(o_made, 1)
                    if inside or 0 <= t < TILES:
                        dve.wait_ge(proj_made, t + 1)
                        dve.wait_ge(x_in[h], 16 * pair + 16)
                        dve.tensor_tensor(y[:, h, :], y_ps[h][:, 0:D], x[:, h, :], ALU.add).then_inc(y_made, 1)
                    if inside or t >= 1:
                        dve.wait_ge(rstd_made, t)
                        if inside or t >= 3:
                            dve.wait_ge(out_done[h1], 16 * (pair if h else pair - 1))
                        dve.tensor_scalar(res[:, h1, :], y[:, h1, :], mv[:, h1, 0:1], rstd[:, h1, :],
                                          ALU.subtract, ALU.mult).then_inc(res_made, 1)
                    if inside or 0 <= t < TILES:
                        dve.wait_ge(y_made, t + 1)
                        dve.bn_stats(stats[:, h, :], y[:, h, :]).then_inc(stats_made, 1)
                    if inside or 0 <= t + 3 < TILES:
                        dve.tensor_scalar(z[:, h1, :].unsqueeze(2), of(t + 3)[:, :, HD:HD + 1], 1e-30, None, ALU.max).then_inc(zmax, 1)
                    if inside or 0 <= t < TILES:
                        dve.wait_ge(eps_set, 1)
                        dve.wait_ge(stats_made, t + 1)
                        dve.bn_aggr(mv[:, h, :], stats[:, h, :]).then_inc(mv_made, 1)

                dve.memset(eps_sb[:, :], EPS).then_inc(eps_set, 1)
                bodies = (TILES - 3) // 4
                for t in range(-3, 4):
                    at_tile(t, t % 2, t // 2)
                with dve.Fori(1, bodies) as i:
                    for j in range(4):
                        at_tile(i * 4 + j, j % 2, i * 2 + j // 2)
                for t in range(4 * bodies, TILES + 1):
                    at_tile(t, t % 2, t // 2)

            @block.tensor
            def _(pe):
                def turn(t, h):
                    pe.wait_ge(o_made, t + 1)
                    for kc in range(2):
                        last = pe.transpose(oT_ps[h][:, kc * P:(kc + 1) * P], o[:, h, kc * P:(kc + 1) * P], ident[:, :])
                    last.then_inc(oT_made, 1)

                def project(t, h, first=False):
                    pe.wait_ge(oT_staged, t + 1)
                    if not first:
                        pe.wait_ge(y_made, t - 1)
                    for kc in range(2):
                        pe.matmul(y_ps[h][:, 0:D], oT[:, h, kc * P:(kc + 1) * P], wo_sb[:, kc, :], start=kc == 0, stop=False)
                    pe.matmul(y_ps[h][:, 0:D], ones_b[:, :], bias_parts[:, PW:BW], start=False, stop=True).then_inc(proj_made, 1)

                turn(0, 0)
                turn(1, 1)
                for h in range(2):
                    project(h, h, first=True)
                    turn(2 + h, h)
                with pe.Fori(1, TILES // 2 - 1) as i:
                    for h in range(2):
                        project(2 * i + h, h)
                        turn(2 * i + 2 + h, h)
                for h in range(2):
                    project(TILES - 2 + h, h)

            @block.scalar
            def _(act):
                def deviation(t, h):
                    act.wait_ge(mv_made, t + 1)
                    act.activation(rstd[:, h, :], mv[:, h, 1:2], ACT.Sqrt, bias=eps_sb[:, :]).then_inc(std_made, 1)

                act.wait_ge(eps_set, 1)
                with act.Fori(0, TILES // 2) as i:
                    for h in range(2):
                        deviation(2 * i + h, h)

            @block.gpsimd
            def _(pool):
                for t in range(-2, TILES + 1):
                    if t + 2 < TILES:
                        if t >= 0:
                            pool.wait_ge(y_made, t + 1)
                        pool.indirect_dma_start(out=x[:, t % 2, :], out_offset=None, in_=x_rows,
                                                in_offset=bass.IndirectOffsetOnAxis(ap=node_id[:, t + 2:t + 3], axis=0),
                                                bounds_check=NP - 1, oob_is_err=False).then_inc(x_in[t % 2], 16)
                    if t >= 1:
                        pool.wait_ge(res_made, t)
                        pool.indirect_dma_start(out=out, out_offset=bass.IndirectOffsetOnAxis(ap=node_id[:, t - 1:t], axis=0),
                                                in_=res[:, (t - 1) % 2, :], in_offset=None,
                                                bounds_check=N - 1, oob_is_err=False).then_inc(out_done[(t - 1) % 2], 16)
                for h in range(2):
                    pool.wait_ge(out_done[h], 16 * TILES // 2)




def kernel(x, src, dst, L0_gnn_Wq, L0_gnn_bq, L0_gnn_Wk, L0_gnn_bk, L0_gnn_Wv, L0_gnn_bv, L0_gnn_Wo, L0_gnn_bo):
    import numpy as np
    import concourse.bacc as bacc
    from concourse.bass_utils import run_bass_kernel_spmd

    by_head = np.arange(D).reshape(HD, HEADS).T.reshape(-1)

    def contraction_first(w):
        return np.ascontiguousarray(np.asarray(w).reshape(2, P, -1).transpose(1, 0, 2))

    rows = np.zeros((NP, D), np.float32)
    rows[:N] = np.asarray(x)
    wq, wk, wv = (np.asarray(w)[by_head].T for w in (L0_gnn_Wq, L0_gnn_Wk, L0_gnn_Wv))
    arrays = {
        "x_rows": rows,
        "xT": contraction_first(rows.T),
        "src": np.ascontiguousarray(np.asarray(src).reshape(EP, EF)),
        "dst": np.ascontiguousarray(np.asarray(dst).reshape(EP, EF)),
        "wT": contraction_first(np.concatenate([wk, wv, wq], 1)),
        "bias": np.concatenate([np.asarray(b)[by_head] for b in (L0_gnn_bk, L0_gnn_bv, L0_gnn_bq)]
                               + [np.asarray(L0_gnn_bo)])[None],
        "woT": contraction_first(np.asarray(L0_gnn_Wo)[:, by_head].T),
    }
    nc = bacc.Bacc("TRN2", target_bir_lowering=False, num_devices=1)
    args = [nc.dram_tensor(f"in_{name}", a.shape, mybir.dt.from_np(a.dtype), kind="ExternalInput").ap() for name, a in arrays.items()]
    out = nc.dram_tensor("out_rows", (N, D), F32, kind="ExternalOutput").ap()
    gnn_kernel(nc, *args, out)
    r = run_bass_kernel_spmd(nc, [{f"in_{name}": a for name, a in arrays.items()}], core_ids=[0])
    return r.results[0]["out_rows"]
```
